# Optimizing a Trainium2 kernel written in Bass

```python
import numpy as np
import jax
import jax.numpy as jnp

def _softmax(x, axis=-1):
    return jax.nn.softmax(x, axis=axis)
def _gelu(x):
    return jax.nn.gelu(x, approximate=True)
def _silu(x):
    return jax.nn.silu(x)
def _sigmoid(x):
    return jax.nn.sigmoid(x)
def _layernorm(x, axis=-1, eps=1e-5):
    m = jnp.mean(x, axis=axis, keepdims=True)
    v = jnp.var(x, axis=axis, keepdims=True)
    return (x - m) / jnp.sqrt(v + eps)
def _scatter_add(tgt, idx, src, axis=0):
    return tgt.at[idx].add(src)
def _segment_sum(src, seg, n):
    return jax.ops.segment_sum(src, seg, n)

kernel_name = 'mk_adj_resnorm_d1_adj_64_b69400'

def setup_inputs(seed: int = 0):
    np.random.seed(seed)
    _w = jnp.asarray
    def _rec_inputs():
        import jax
        import jax.numpy as jnp
        _gk = jax.random.key(seed)
        x = -9.806e-05 + 1 * jax.random.normal(jax.random.fold_in(_gk, 1), (8192, 64), jnp.float32)
        _a = jax.random.bernoulli(jax.random.fold_in(_gk, 2), 0.000488281, (8192, 8192))
        _a = jnp.logical_or(_a, jnp.swapaxes(_a, -1, -2))
        _a = jnp.logical_or(_a, jnp.eye(8192, dtype=bool))
        adj = _a.astype(jnp.int32)
        return x, adj
    x, adj = _rec_inputs()
    def _L0_gnn_setup():
        import jax, jax.numpy as jnp
        import numpy as np
        ALPHA = 0.2
        NEG_BIG = -9000000000000000.0
        key = jax.random.key(seed)
        k1, k2, k3, k4, k5 = jax.random.split(key, 5)
        N, M, F_in, F_out = (8192, 8192, 64, 64)
        item_embs = jax.random.normal(k1, (N, F_in), dtype=jnp.float32)
        entity_embs = jax.random.normal(k2, (M, F_in), dtype=jnp.float32)
        adj = jax.random.randint(k3, (N, M), 0, 2, dtype=jnp.int32)
        W = jax.random.normal(k4, (F_in, F_out), dtype=jnp.float32)
        a = jax.random.normal(k5, (2 * F_out, 1), dtype=jnp.float32)
        return {'item_embs': item_embs, 'entity_embs': entity_embs, 'adj': adj, 'W': W, 'a': a}
    _L0_gnn_all = _L0_gnn_setup()
    _L0_gnn_in = {k: v for k, v in _L0_gnn_all.items() if k in ('entity_embs', 'W', 'a', )}
    del _L0_gnn_all

    return {
        "x": x,
        "adj": adj,
        "L0_gnn_entity_embs": _L0_gnn_in["entity_embs"],
        "L0_gnn_W": _L0_gnn_in["W"],
        "L0_gnn_a": _L0_gnn_in["a"],
    }

def reference(x, adj, L0_gnn_entity_embs, L0_gnn_W, L0_gnn_a):
    import jax
    import jax.numpy as jnp
    def _L0_gnn_ref(item_embs, entity_embs, adj, W, a):
        import jax, jax.numpy as jnp
        import numpy as np
        ALPHA = 0.2
        NEG_BIG = -9000000000000000.0
        F_out = W.shape[1]
        Wh = item_embs @ W
        We = entity_embs @ W
        a1 = a[:F_out, 0]
        a2 = a[F_out:, 0]
        scores = (Wh @ a1)[:, None] + (We @ a2)[None, :]
        e = jnp.where(scores > 0, scores, ALPHA * scores)
        e = jnp.where(adj > 0, e, NEG_BIG)
        attention = jax.nn.softmax(e, axis=1)
        entity_emb_weighted = attention @ entity_embs
        h_prime = entity_emb_weighted + item_embs
        return jax.nn.elu(h_prime)

    x = _layernorm(x + _L0_gnn_ref(x, L0_gnn_entity_embs, adj, L0_gnn_W, L0_gnn_a), axis=-1)
    return x


_drawn_inputs = setup_inputs


def setup_inputs(seed=0):
    import zlib

    import numpy as np

    out = dict(_drawn_inputs(seed))
    spreads = {}
    factors = {}
    for name, (base, spread) in spreads.items():
        noise = np.random.default_rng([zlib.crc32(name.encode()), seed]).standard_normal(out[name].shape)
        drawn = base * np.exp(spread * noise) if base else spread * noise
        out[name] = jnp.asarray(drawn.astype(out[name].dtype))
    for name, factor in factors.items():
        out[name] = (out[name] * factor).astype(out[name].dtype)
    return out
```

```python
from contextlib import ExitStack

import concourse.bass as bass
from concourse import mybir

ALU = mybir.AluOpType
ACT = mybir.ActivationFunctionType
AX_X = mybir.AxisListType.X
F32 = mybir.dt.float32
BF16 = mybir.dt.bfloat16
I32 = mybir.dt.int32

P = 128
ROWS_PER_SB = 512
RB = ROWS_PER_SB // P
GROUP_COLS = 2048
GT = GROUP_COLS // P
SLOTS = 6
MASKED = -(2.0 ** 100)
NO_MAX = -3.0e38
ALPHA = 0.2
EPS = 1e-5
LEAD = 5
X_BUFS = 3
CYCLE = 3

ORDER = "ADADAADADA"
ITEMS = []
for _kind in ORDER:
    _first = sum(2 if k == "A" else 1 for k, _, _ in ITEMS)
    ITEMS.append((_kind, _first, sum(1 for k, _, _ in ITEMS if k == _kind)))
NI = len(ITEMS)
NA = ORDER.count("A")
ND = ORDER.count("D")
assert 2 * NA + ND == GT and NA % 2 == 0 and ND == RB
SPREAD_S_AT, SPREAD_V_AT, KEEP_S_AT = 5, 8, 3


def item_before(kind, nth, back):
    count = NA if kind == "A" else ND
    wrapped = (nth - back) % count
    where = [i for i, (k, _, q) in enumerate(ITEMS) if k == kind and q == wrapped][0]
    return where + NI * ((nth - back) // count)


def build_gat_layer(nc, x, adj, ent, W, a, out):
    N, M = adj.shape
    F = W.shape[0]
    FA = F + 1
    JT = M // P
    G = M // GROUP_COLS
    SB = N // ROWS_PER_SB
    assert W.shape[1] == F and N == SB * ROWS_PER_SB and M == G * GROUP_COLS

    with ExitStack() as ctx:
        def sb_t(name, shape, dt=F32):
            return ctx.enter_context(nc.sbuf_tensor(name, shape, dt))

        def sem(name):
            return ctx.enter_context(nc.semaphore(name))

        adj_in = sb_t("adj_in", [P, RB, GROUP_COLS], I32)
        mask = sb_t("mask", [P, SLOTS, RB, GROUP_COLS], BF16)
        t_row = sb_t("t_row", [P, M], BF16)
        ent_aug = sb_t("ent_aug", [P, JT, FA])
        probs_a = sb_t("probs_a", [P, 2, 2 * ROWS_PER_SB])
        probs_d = sb_t("probs_d", [P, 2, ROWS_PER_SB])
        s_row = sb_t("s_row", [P, 2, ROWS_PER_SB])
        v_row = sb_t("v_row", [P, 2, ROWS_PER_SB])
        sv_row = sb_t("sv_row", [P, 2, ROWS_PER_SB])
        x_sb = sb_t("x_sb", [P, X_BUFS, RB, F])
        t_col = sb_t("t_col", [P, JT])
        t_hi = sb_t("t_hi", [P, JT])
        t_lo = sb_t("t_lo", [P, JT])
        ident = sb_t("ident", [P, P])
        ident_bf = sb_t("ident_bf", [P, P], BF16)
        ones = sb_t("ones", [P, P])
        ones_bf = sb_t("ones_bf", [P, P], BF16)
        zeros_bf = sb_t("zeros_bf", [P, ROWS_PER_SB], BF16)
        w_in = sb_t("w_in", [F, F])
        w_t = sb_t("w_t", [F, F])
        a_in = sb_t("a_in", [F, 2])
        a_rep = sb_t("a_rep", [F, 2, P])
        wa = sb_t("wa", [P, 2, F])
        ent_sum = sb_t("ent_sum", [P, FA])
        diag = sb_t("diag", [P, 2, ROWS_PER_SB])
        v_diag = sb_t("v_diag", [P, 2, ROWS_PER_SB], BF16)
        s_col = sb_t("s_col", [P, RB])
        t_max_part = sb_t("t_max_part", [P, RB, G])
        t_max = sb_t("t_max", [P, RB])
        top = sb_t("top", [P, RB])
        guard = sb_t("guard", [P, RB])
        v_col = sb_t("v_col", [P, RB])
        no_edge = sb_t("no_edge", [P, 3, RB])
        dot_junk = sb_t("dot_junk", [P, RB, F])
        sums = sb_t("sums", [P, RB, FA])
        inv_den = sb_t("inv_den", [P, RB])
        h = sb_t("h", [P, RB, F])
        h_neg = sb_t("h_neg", [P, RB, F])
        y = sb_t("y", [P, RB, F])
        stat = sb_t("stat", [P, 6, RB])
        rstd_guess = sb_t("rstd_guess", [P, RB])
        minus_half = sb_t("minus_half", [P, RB])
        res = sb_t("res", [P, 2, RB, F])

        z_a = ctx.enter_context(nc.psum_tensor("z_a", [P, 2, 2 * ROWS_PER_SB], F32))
        z_d = ctx.enter_context(nc.psum_tensor("z_d", [P, 2, ROWS_PER_SB], F32))
        acc = ctx.enter_context(nc.psum_tensor("acc", [P, 512], F32))
        misc = ctx.enter_context(nc.psum_tensor("misc", [P, 512], F32))
        acc_rb = acc[:, 0:RB * FA].rearrange("p (r f) -> p r f", r=RB)

        small_in = sem("small_in")
        ent_in = sem("ent_in")
        x_in = sem("x_in")
        adj_arrived = [sem(f"adj_arrived{r}") for r in range(RB)]
        pool_done = sem("pool_done")
        consts_made = sem("consts_made")
        setup_pe = sem("setup_pe")
        setup_dve = sem("setup_dve")
        setup_self = sem("setup_self")
        v_kept = sem("v_kept")
        t_diag_made = sem("t_diag_made")
        t_spread = sem("t_spread")
        t_row_made = sem("t_row_made")
        ent_summed = sem("ent_summed")
        banks_marked = sem("banks_marked")
        mask_made = sem("mask_made")
        max_made = sem("max_made")
        guard_made = sem("guard_made")
        s_spread = sem("s_spread")
        s_kept = sem("s_kept")
        guard_step = sem("guard_step")
        sums_step = sem("sums_step")
        finish_step = sem("finish_step")
        var_made = sem("var_made")
        rstd_guessed = sem("rstd_guessed")
        v_spread = sem("v_spread")
        rows_made = sem("rows_made")
        z_a_written = sem("z_a_written")
        z_d_written = sem("z_d_written")
        z_masked = sem("z_masked")
        probs_made = sem("probs_made")
        probs_used = sem("probs_used")
        acc_done = sem("acc_done")
        acc_taken = sem("acc_taken")
        h_made = sem("h_made")
        elu_made = sem("elu_made")
        res_made = sem("res_made")
        out_done = sem("out_done")
        res_stored = sem("res_stored")

        x_tiles = x.rearrange("(s r p) f -> s p r f", r=RB, p=P)
        out_tiles = out.rearrange("(s r p) f -> s p r f", r=RB, p=P)
        scratch = mask[:, SLOTS - 1].bitcast(F32)
        scratch = scratch.rearrange("p r c -> p (r c)")[:, 0:JT * F].rearrange("p (t f) -> p t f", f=F)
        T_SPREADS = JT // RB

        assert (CYCLE * G) % SLOTS == 0 and CYCLE % X_BUFS == 0 and (SB - 4) % CYCLE == 0
        block = ctx.enter_context(nc.Block())

        def pick(tensor, index):
            names = " ".join("abc"[:len(tensor.shape) - 2])
            return tensor[:, bass.ds(index, 1)].rearrange(f"p o {names} -> p (o {names[0]}) {names[1:]}"
                                                          if names else "p o -> p o")

        def wait_apart(engine, *waits):
            values = [(signal, engine.to_reg(value)) for signal, value in waits]
            engine.wait_ge(pool_done, 3)
            for signal, value in values:
                engine.wait_ge(signal, value)

        @block.sync
        def _(sp):
            sp.dma_start(w_in[:], W).then_inc(small_in, 16)
            for c in range(2):
                sp.dma_start(a_in[:, c:c + 1], a[c * F:(c + 1) * F, :]).then_inc(small_in, 16)
            sp.dma_start(ent_aug[:, :, 0:F], ent.rearrange("(t p) f -> p t f", p=P)).then_inc(ent_in, 16)

            def load_group(s, g, fresh=False):
                n = s * G + g
                for r in range(RB):
                    if not fresh:
                        sp.wait_ge(max_made, n * RB + (r + 1 - RB))
                    sp.dma_start(adj_in[:, r, :],
                                 adj[bass.ds((s * RB + r) * P, P), bass.ds(g * GROUP_COLS, GROUP_COLS)]
                                 ).then_inc(adj_arrived[r], 16)

            def load_x(s):
                sp.dma_start(pick(x_sb, s % X_BUFS), x_tiles[bass.ds(s, 1)].rearrange("o p r f -> p (o r) f")
                             ).then_inc(x_in, 16)

            load_group(0, 0, fresh=True)
            sp.dma_start(x_sb[:, 0], x_tiles[0]).then_inc(x_in, 16)
            with sp.Fori(1, G) as g:
                load_group(0, g)
            with sp.Fori(1, X_BUFS) as s:
                with sp.Fori(0, G) as g:
                    load_group(s, g)
                wait_apart(sp, (x_in, s * 16))
                load_x(s)
            with sp.Fori(X_BUFS, SB) as s:
                with sp.Fori(0, G) as g:
                    load_group(s, g)
                wait_apart(sp, (x_in, s * 16), (res_made, s - (X_BUFS - 1)))
                load_x(s)

        @block.gpsimd
        def _(pool):
            nc.gpsimd.memset(ident[:], 0.0).then_inc(pool_done, 1)
            nc.gpsimd.memset(minus_half[:], -0.5).then_inc(pool_done, 1)
            pool.wait_ge(pool_done, 2)
            nc.gpsimd.affine_select(out=ident[:], in_=ident[:], compare_op=ALU.not_equal, fill=1.0, base=0,
                                    pattern=[[-1, P]], channel_multiplier=1).then_inc(pool_done, 1)
            pool.sem_inc(res_stored, 1)
            with pool.Fori(0, SB) as s:
                pool.wait_ge(var_made, s + 1)
                nc.gpsimd.tensor_tensor(rstd_guess[:], stat[:, 2, :], minus_half[:], ALU.pow
                                        ).then_inc(rstd_guessed, 1)
                pool.wait_ge(res_made, s + 1)
                pool.dma_start(out_tiles[bass.ds(s, 1)].rearrange("o p r f -> p (o r) f"),
                               pick(res, s % 2)).then_inc(out_done, 16)
                pool.wait_ge(out_done, s * 16 + 16)
                pool.sem_inc(res_stored, 1)

        @block.scalar
        def _(act):
            for q in range(T_SPREADS):
                act.wait_ge(t_spread, q + 1)
                nc.scalar.activation(t_row[:, q * ROWS_PER_SB:(q + 1) * ROWS_PER_SB], z_a[:, q % 2, 0:ROWS_PER_SB],
                                     ACT.Copy).then_inc(t_row_made, 1)

            def leaky(s, g, k):
                _, first, nth = ITEMS[k]
                n = s * G + g
                wait_apart(act, (probs_made, n * NI + (NI + item_before("A", nth, 2) + 1)))
                for u in range(2):
                    ins = nc.scalar.activation(z_a[:, nth % 2, u * ROWS_PER_SB:(u + 1) * ROWS_PER_SB],
                                               pick(s_row, s % 2), ACT.Relu,
                                               bias=t_hi[:, bass.ds(g * GT + (first + u), 1)])
                ins.then_inc(z_a_written, 1)

            def exponential(s, g, k):
                kind, first, nth = ITEMS[k]
                n = s * G + g
                wait_apart(act, (z_masked, n * NI + (SLOTS * NI + k + 1)),
                           (probs_used, n * NI + (NI + item_before(kind, nth, 2) + 1)))
                z, probs = (z_a, probs_a) if kind == "A" else (z_d, probs_d)
                for u in range(2 if kind == "A" else 1):
                    cols = slice(u * ROWS_PER_SB, (u + 1) * ROWS_PER_SB)
                    ins = nc.scalar.activation(probs[:, nth % 2, cols], z[:, nth % 2, cols], ACT.Exp,
                                               bias=t_lo[:, bass.ds(g * GT + (first + u), 1)])
                ins.then_inc(probs_made, 1)

            def group(s, g, following=None):
                for k in range(1, NI):
                    if ITEMS[k][0] == "A":
                        leaky(s, g, k)
                    exponential(s, g, k - 1)
                if following is not None:
                    leaky(*following, 0)
                exponential(s, g, NI - 1)

            def elu(s):
                act.wait_ge(h_made, s + 1)
                nc.scalar.activation(h_neg[:], h_neg[:], ACT.Exp).then_inc(elu_made, 1)

            def superblock(s, first=False, last=False):
                group(s, 0, (s, 1))
                if not first:
                    elu(s - 1)
                with act.Fori(1, G - 1) as g:
                    group(s, g, (s, g + 1))
                if last:
                    group(s, G - 1)
                else:
                    for k in range(1, NI):
                        if ITEMS[k][0] == "A":
                            leaky(s, G - 1, k)
                        exponential(s, G - 1, k - 1)
                    act.wait_ge(rows_made, s + 2)
                    leaky(s + 1, 0, 0)
                    exponential(s, G - 1, NI - 1)

            act.sem_inc(probs_made, NI)
            act.wait_ge(banks_marked, 1)
            act.wait_ge(rows_made, 1)
            leaky(0, 0, 0)
            superblock(0, first=True)
            with act.Fori(1, SB - 1) as s:
                superblock(s)
            superblock(SB - 1, last=True)
            elu(SB - 1)

        @block.tensor
        def _(pe):
            pe.wait_ge(small_in, 48)
            pe.wait_ge(consts_made, 1)
            pe.transpose(misc[0:F, 0:F], w_in[:], ident[0:F, 0:F]).then_inc(setup_pe, 1)
            pe.wait_ge(setup_dve, 1)
            for c in range(2):
                mm = pe.matmul(misc[:, c * F:(c + 1) * F], a_rep[:, c, :], w_t[:], start=True, stop=True)
            mm.then_inc(setup_pe, 1)
            for q in range(T_SPREADS):
                pe.wait_ge(t_diag_made, q + 1)
                if q >= 2:
                    pe.wait_ge(t_row_made, q - 1)
                pe.matmul(z_a[:, q % 2, 0:ROWS_PER_SB], ones[:], diag[:, q % 2, :], start=True, stop=True
                          ).then_inc(t_spread, 1)
            for t in range(JT):
                mm = pe.matmul(acc[:, 0:FA], ones[:], ent_aug[:, t, :], start=(t == 0), stop=(t == JT - 1))
            mm.then_inc(ent_summed, 1)
            pe.wait_ge(t_row_made, T_SPREADS)
            for half in range(2):
                for b in range(2):
                    pe.matmul(z_a[:, half, b * ROWS_PER_SB:(b + 1) * ROWS_PER_SB], zeros_bf[:, 0:P], zeros_bf[:],
                              start=True, stop=True)
                mm = pe.matmul(z_d[:, half, :], zeros_bf[:, 0:P], zeros_bf[:], start=True, stop=True)
            mm.then_inc(banks_marked, 1)

            def add_mask(s, g, k):
                kind, first, nth = ITEMS[k]
                n = s * G + g
                if kind == "A":
                    pe.wait_ge(z_a_written, n * NA + (nth + 1))
                    banks = [z_a[:, nth % 2, 0:ROWS_PER_SB], z_a[:, nth % 2, ROWS_PER_SB:2 * ROWS_PER_SB]]
                else:
                    pe.wait_ge(z_d_written, n * ND + (nth + 1))
                    banks = [z_d[:, nth % 2, :]]
                slot = pick(mask, n % SLOTS)
                for u, z in enumerate(banks):
                    for r in range(RB):
                        mm = pe.matmul(z[:, r * P:(r + 1) * P], slot[:, r, (first + u) * P:(first + u + 1) * P],
                                       ident_bf[:], start=False, stop=True, skip_group_check=True)
                if kind == "A":
                    for z in banks:
                        mm = pe.matmul(z, ones_bf[:], pick(v_diag, s % 2),
                                       start=False, stop=True, skip_group_check=True)
                mm.then_inc(z_masked, 1)

            def weigh(s, g, k):
                kind, first, nth = ITEMS[k]
                n = s * G + g
                pe.wait_ge(probs_made, n * NI + (NI + k + 1))
                for u in range(2 if kind == "A" else 1):
                    for r in range(RB):
                        c = (u * RB + r) * P
                        lhs = probs_a[:, nth % 2, c:c + P] if kind == "A" else probs_d[:, nth % 2, c:c + P]
                        mm = pe.matmul(acc_rb[:, r, :], lhs, pick(ent_aug, g * GT + (first + u)),
                                       start=False, stop=True, skip_group_check=True)
                mm.then_inc(probs_used, 1)

            def spread_s(s):
                pe.wait_ge(guard_made, s + 1)
                pe.matmul(misc[:], ones[:], diag[:, 0, :], start=True, stop=True).then_inc(s_spread, 1)

            def spread_v(s):
                pe.wait_ge(s_kept, s + 1)
                pe.matmul(misc[:], ones_bf[:], pick(v_diag, s % 2), start=True, stop=True).then_inc(v_spread, 1)

            def clear_acc(s):
                pe.wait_ge(acc_taken, s + 1)
                pe.matmul(acc[:, 0:RB * FA], zeros_bf[:, 0:P], zeros_bf[:, 0:RB * FA], start=True, stop=True)

            def superblock(s, last=False):
                add_mask(s, 0, 1)
                clear_acc(s)
                weigh(s, 0, 0)
                for k in range(2, NI):
                    add_mask(s, 0, k)
                    weigh(s, 0, k - 1)
                add_mask(s, 1, 0)
                weigh(s, 0, NI - 1)
                with pe.Fori(1, G - 1) as g:
                    for k in range(1, NI):
                        add_mask(s, g, k)
                        weigh(s, g, k - 1)
                    add_mask(s, g + 1, 0)
                    weigh(s, g, NI - 1)
                for k in range(1, NI):
                    add_mask(s, G - 1, k)
                    weigh(s, G - 1, k - 1)
                    if not last and k == SPREAD_S_AT:
                        spread_s(s + 1)
                    if not last and k == SPREAD_V_AT:
                        spread_v(s + 1)
                if not last:
                    add_mask(s + 1, 0, 0)
                weigh(s, G - 1, NI - 1)

            pe.sem_inc(z_masked, SLOTS * NI)
            pe.sem_inc(probs_used, NI)
            spread_s(0)
            spread_v(0)
            add_mask(0, 0, 0)
            superblock(0)
            with pe.Fori(1, SB - 1) as s:
                superblock(s)
            superblock(SB - 1, last=True)

        @block.vector
        def _(dve):
            nc.vector.memset(ones[:], 1.0).then_inc(setup_self, 1)
            nc.vector.memset(ones_bf[:], 1.0).then_inc(setup_self, 1)
            nc.vector.memset(zeros_bf[:], 0.0).then_inc(setup_self, 1)
            nc.vector.memset(ent_aug[:, :, F:FA], 1.0).then_inc(setup_self, 1)
            dve.wait_ge(pool_done, 3)
            nc.vector.tensor_copy(ident_bf[:], ident[:]).then_inc(setup_self, 1)
            dve.wait_ge(setup_self, 5)
            dve.sem_inc(consts_made, 1)
            dve.wait_ge(small_in, 48)
            for c in range(2):
                nc.vector.tensor_scalar(a_rep[:, c, :], ones[0:F, :], a_in[:, c:c + 1], None, ALU.mult
                                        ).then_inc(setup_self, 1)
            dve.wait_ge(setup_pe, 1)
            dve.wait_ge(setup_self, 7)
            nc.vector.tensor_copy(w_t[:], misc[0:F, 0:F]).then_inc(setup_dve, 1)
            dve.wait_ge(setup_pe, 2)
            nc.vector.tensor_copy(wa[:].rearrange("p c f -> p (c f)"), misc[:, 0:2 * F]).then_inc(setup_dve, 1)
            dve.wait_ge(ent_in, 16)
            dve.wait_ge(setup_dve, 2)
            nc.vector.tensor_tensor(scratch, ent_aug[:, :, 0:F],
                                    wa[:, 1:2, :].broadcast_to([P, JT, F]), ALU.mult).then_inc(setup_dve, 1)
            dve.wait_ge(setup_dve, 3)
            nc.vector.tensor_reduce(t_col[:], scratch, AX_X, ALU.add).then_inc(setup_dve, 1)
            dve.wait_ge(setup_dve, 4)
            nc.vector.tensor_scalar(t_hi[:], t_col[:], 1.0 - ALPHA, None, ALU.mult).then_inc(setup_dve, 1)
            nc.vector.tensor_scalar(t_lo[:], t_col[:], ALPHA, None, ALU.mult).then_inc(setup_dve, 1)
            for q in range(T_SPREADS):
                if q >= 2:
                    dve.wait_ge(t_spread, q - 1)
                for c in range(RB):
                    ins = nc.vector.tensor_scalar(diag[:, q % 2, c * P:(c + 1) * P], ident[:],
                                                  t_col[:, RB * q + c:RB * q + c + 1], None, ALU.mult)
                ins.then_inc(t_diag_made, 1)
            dve.wait_ge(ent_summed, 1)
            nc.vector.tensor_copy(ent_sum[:], acc[:, 0:FA]).then_inc(acc_taken, 1)
            dve.wait_ge(t_row_made, T_SPREADS)

            def make_mask(s, phase, g, r, fresh=False):
                n = s * G + g
                dve.wait_ge(adj_arrived[r], n * 16 + 16)
                if not fresh:
                    dve.wait_ge(z_masked, n * NI + NI)
                slot = mask[:, (phase * G + g) % SLOTS, r, :]
                nc.vector.tensor_scalar(slot, adj_in[:, r, :], 0.0, MASKED, ALU.is_le, ALU.mult
                                        ).then_inc(mask_made, 1)
                wait_apart(dve, (mask_made, n * RB + (r + 1)))
                spent = adj_in[:, r, :].bitcast(BF16)[:, 0:GROUP_COLS]
                nc.vector.tensor_tensor_reduce(spent, slot, t_row[:, g * GROUP_COLS:(g + 1) * GROUP_COLS],
                                               1.0, NO_MAX, ALU.add, ALU.max,
                                               t_max_part[:, r, g:g + 1]).then_inc(max_made, 1)

            def leaky(s, g, nth):
                first = [q[1] for q in ITEMS if q[0] == "D"][nth]
                n = s * G + g
                dve.wait_ge(probs_made, n * NI + (NI + item_before("D", nth, 2) + 1))
                nc.vector.scalar_tensor_tensor(out=z_d[:, nth % 2, :], in0=pick(sv_row, s % 2),
                                               scalar=t_hi[:, bass.ds(g * GT + first, 1)], in1=pick(v_row, s % 2),
                                               op0=ALU.add, op1=ALU.max).then_inc(z_d_written, 1)

            def chain(signal, rounds_done, steps):
                taken = []

                def then(ins):
                    taken.append(1)
                    assert len(taken) <= steps
                    ins.then_inc(signal, 1)
                    dve.wait_ge(signal, rounds_done * steps + len(taken))

                return then

            def make_guard(s, phase):
                then = chain(guard_step, s, 5)
                wait_apart(dve, (x_in, s * 16 + 16))
                xs = x_sb[:, phase % X_BUFS]
                for r in range(RB):
                    ins = nc.vector.tensor_tensor_reduce(dot_junk[:, r, :], xs[:, r, :], wa[:, 0, :], 1.0, 0.0,
                                                         ALU.mult, ALU.add, s_col[:, r:r + 1])
                then(ins)
                for r in range(RB):
                    nc.vector.tensor_scalar(diag[:, 0, r * P:(r + 1) * P], ident[:], s_col[:, r:r + 1], 1.0 - ALPHA,
                                            ALU.mult, ALU.mult)
                dve.wait_ge(max_made, s * (G * RB) + G * RB)
                then(nc.vector.tensor_reduce(t_max[:], t_max_part[:], AX_X, ALU.max))
                nc.vector.tensor_scalar(pick(no_edge, s % 3), t_max[:], MASKED / 2, None, ALU.is_lt)
                then(nc.vector.tensor_tensor(top[:], t_max[:], s_col[:], ALU.add))
                then(nc.vector.scalar_tensor_tensor(out=guard[:], in0=top[:], scalar=ALPHA, in1=top[:],
                                                    op0=ALU.mult, op1=ALU.max))
                then(nc.vector.scalar_tensor_tensor(out=v_col[:], in0=s_col[:], scalar=ALPHA, in1=guard[:],
                                                    op0=ALU.mult, op1=ALU.subtract))
                for r in range(RB):
                    ins = nc.vector.tensor_scalar(pick(v_diag, s % 2)[:, r * P:(r + 1) * P],
                                                  ident_bf[:], v_col[:, r:r + 1], None, ALU.mult)
                ins.then_inc(guard_made, 1)

            def keep_s(s):
                dve.wait_ge(s_spread, s + 1)
                nc.vector.tensor_copy(pick(s_row, s % 2), misc[:]).then_inc(s_kept, 1)

            def keep_v(s):
                dve.wait_ge(v_spread, s + 1)
                nc.vector.tensor_copy(pick(v_row, s % 2), misc[:]).then_inc(v_kept, 1)
                dve.wait_ge(v_kept, s + 1)
                nc.vector.tensor_tensor(pick(sv_row, s % 2), pick(s_row, s % 2), pick(v_row, s % 2), ALU.add
                                        ).then_inc(rows_made, 1)
                dve.wait_ge(rows_made, s + 1)

            def take_sums(s):
                then = chain(sums_step, s, 2)
                xs = pick(x_sb, s % X_BUFS)
                ne = pick(no_edge, s % 3)
                dve.wait_ge(probs_used, s * (G * NI) + (G * NI + NI))
                for r in range(RB):
                    ins = nc.vector.scalar_tensor_tensor(out=sums[:, r, :], in0=ent_sum[:], scalar=ne[:, r:r + 1],
                                                         in1=acc_rb[:, r, :], op0=ALU.mult, op1=ALU.add)
                ins.then_inc(acc_taken, 1)
                dve.wait_ge(acc_taken, s + 2)
                then(nc.vector.reciprocal(inv_den[:], sums[:, :, F]))
                for r in range(RB):
                    ins = nc.vector.scalar_tensor_tensor(out=h[:, r, :], in0=sums[:, r, 0:F], scalar=inv_den[:, r:r + 1],
                                                         in1=xs[:, r, :], op0=ALU.mult, op1=ALU.add)
                then(ins)
                nc.vector.tensor_scalar(h_neg[:], h[:], 0.0, None, ALU.min).then_inc(h_made, 1)

            def finish(s, first=False):
                then = chain(finish_step, s, 11)
                xs = pick(x_sb, s % X_BUFS)
                mean, ss, var, half, g2, rstd = (stat[:, q, :] for q in range(6))
                then(nc.vector.tensor_scalar(y[:], h[:], 0.0, -1.0, ALU.max, ALU.add))
                then(nc.vector.tensor_tensor(y[:], y[:], xs, ALU.add))
                dve.wait_ge(elu_made, s + 1)
                then(nc.vector.tensor_tensor(y[:], y[:], h_neg[:], ALU.add))
                then(nc.vector.tensor_reduce(ss, y[:], AX_X, ALU.add))
                then(nc.vector.tensor_scalar(mean, ss, 1.0 / F, None, ALU.mult))
                for r in range(RB):
                    ins = nc.vector.tensor_scalar(y[:, r, :], y[:, r, :], mean[:, r:r + 1], None, ALU.subtract)
                then(ins)
                for r in range(RB):
                    ins = nc.vector.tensor_tensor_reduce(dot_junk[:, r, :], y[:, r, :], y[:, r, :], 1.0, 0.0,
                                                         ALU.mult, ALU.add, ss[:, r:r + 1])
                then(ins)
                nc.vector.tensor_scalar(var, ss, 1.0 / F, EPS, ALU.mult, ALU.add).then_inc(var_made, 1)
                dve.wait_ge(rstd_guessed, s + 1)
                then(nc.vector.tensor_tensor(g2, rstd_guess[:], rstd_guess[:], ALU.mult))
                then(nc.vector.tensor_tensor(half, g2, var, ALU.mult))
                then(nc.vector.tensor_scalar(half, half, -0.5, 1.5, ALU.mult, ALU.add))
                then(nc.vector.tensor_tensor(rstd, half, rstd_guess[:], ALU.mult))
                dve.wait_ge(res_stored, s + 1)
                for r in range(RB):
                    ins = nc.vector.tensor_scalar(pick(res, s % 2)[:, r, :], y[:, r, :], rstd[:, r:r + 1], None, ALU.mult)
                ins.then_inc(res_made, 1)

            def group(s, g, made=None, extra=None):
                for nth in range(ND):
                    leaky(s, g, nth)
                    if extra and nth in extra:
                        extra[nth]()
                    if made is not None:
                        make_mask(*made, nth)

            def superblock(s, phase, first=False, ahead=2):
                for g in range(G):
                    extra = {}
                    if g == 0 and not first:
                        extra[0] = lambda: take_sums(s - 1)
                    if g < G - 1:
                        made = (s + 1, (phase + 1) % CYCLE, g + 1) if ahead else None
                    else:
                        made = (s + 2, (phase + 2) % CYCLE, 0) if ahead > 1 else None
                        if ahead:
                            make_guard(s + 1, (phase + 1) % CYCLE)
                            extra[KEEP_S_AT] = lambda: keep_s(s + 1)
                        if not first:
                            finish(s - 1)
                    group(s, g, made, extra)
                if ahead:
                    keep_v(s + 1)

            for g in range(G):
                for r in range(RB):
                    make_mask(0, 0, g, r, fresh=True)
            make_guard(0, 0)
            keep_s(0)
            keep_v(0)
            for r in range(RB):
                make_mask(1, 1, 0, r, fresh=True)
            superblock(0, 0, first=True)
            with dve.Fori(1, SB - 3, CYCLE) as s:
                for c in range(CYCLE):
                    superblock(s + c, (1 + c) % CYCLE)
            superblock(SB - 3, (SB - 3) % CYCLE)
            superblock(SB - 2, (SB - 2) % CYCLE, ahead=1)
            superblock(SB - 1, (SB - 1) % CYCLE, ahead=0)
            take_sums(SB - 1)
            finish(SB - 1)


def kernel(**inputs):
    import numpy as _np
    import concourse.bacc as _bacc
    from concourse.bass_utils import run_bass_kernel_spmd as _run

    names = ["x", "adj", "L0_gnn_entity_embs", "L0_gnn_W", "L0_gnn_a"]
    nc = _bacc.Bacc("TRN2", target_bir_lowering=False, num_devices=1)
    arrays, args = {}, []
    for name in names:
        v = _np.ascontiguousarray(inputs[name])
        arrays[f"in_{name}"] = v
        args.append(nc.dram_tensor(f"in_{name}", v.shape, mybir.dt.from_np(v.dtype), kind="ExternalInput").ap())
    out = nc.dram_tensor("out", inputs["x"].shape, F32, kind="ExternalOutput").ap()
    build_gat_layer(nc, *args, out)
    return _run(nc, [arrays], core_ids=[0]).results[0]["out"]
```

```python
from contextlib import ExitStack

import concourse.bass as bass
from concourse import mybir

ALU = mybir.AluOpType
ACT = mybir.ActivationFunctionType
AX_X = mybir.AxisListType.X
F32 = mybir.dt.float32
BF16 = mybir.dt.bfloat16
I32 = mybir.dt.int32

P = 128
ROWS_PER_SB = 512
RB = ROWS_PER_SB // P
GROUP_COLS = 2048
GT = GROUP_COLS // P
SLOTS = 6
EDGE = 2.0 ** -64
FROM_EDGE = 2.0 ** 64
NO_MAX = -3.0e38
ALPHA = 0.2
EPS = 1e-5
LEAD = 5
X_BUFS = 3
CYCLE = 3

ORDER = "ADADAADADA"
ITEMS = []
for _kind in ORDER:
    _first = sum(2 if k == "A" else 1 for k, _, _ in ITEMS)
    ITEMS.append((_kind, _first, sum(1 for k, _, _ in ITEMS if k == _kind)))
NI = len(ITEMS)
NA = ORDER.count("A")
ND = ORDER.count("D")
assert 2 * NA + ND == GT and NA % 2 == 0 and ND == RB
D_AT = [i for i, (k, _, _) in enumerate(ITEMS) if k == "D"]
SPREAD_S_AT, CLEAR_AT = 1, 8


def item_before(kind, nth, back):
    count = NA if kind == "A" else ND
    wrapped = (nth - back) % count
    where = [i for i, (k, _, q) in enumerate(ITEMS) if k == kind and q == wrapped][0]
    return where + NI * ((nth - back) // count)


def build_gat_layer(nc, x, adj, ent, W, a, out):
    N, M = adj.shape
    F = W.shape[0]
    FA = F + 1
    JT = M // P
    G = M // GROUP_COLS
    SB = N // ROWS_PER_SB
    assert W.shape[1] == F and N == SB * ROWS_PER_SB and M == G * GROUP_COLS

    with ExitStack() as ctx:
        def sb_t(name, shape, dt=F32):
            return ctx.enter_context(nc.sbuf_tensor(name, shape, dt))

        def sem(name):
            return ctx.enter_context(nc.semaphore(name))

        adj_in = sb_t("adj_in", [P, RB, GROUP_COLS], I32)
        mask = sb_t("mask", [P, SLOTS, RB, GROUP_COLS], BF16)
        t_row = sb_t("t_row", [P, M], BF16)
        ent_aug = sb_t("ent_aug", [P, JT, FA])
        probs_a = sb_t("probs_a", [P, 2, 2 * ROWS_PER_SB])
        probs_d = sb_t("probs_d", [P, 2, ROWS_PER_SB])
        s_row = sb_t("s_row", [P, 2, ROWS_PER_SB])
        x_sb = sb_t("x_sb", [P, X_BUFS, RB, F])
        t_col = sb_t("t_col", [P, JT])
        t_hi = sb_t("t_hi", [P, JT])
        t_lo = sb_t("t_lo", [P, JT])
        t_below = sb_t("t_below", [P, JT])
        t_ends_part = sb_t("t_ends_part", [P, 2])
        t_ends_col = sb_t("t_ends_col", [2, 1])
        t_ends_diag = sb_t("t_ends_diag", [2, 2])
        t_ends = sb_t("t_ends", [P, 2])
        t_ref = sb_t("t_ref", [P, 1])
        t_least = sb_t("t_least", [P, 1])
        t_shift = sb_t("t_shift", [P, 1])
        ident = sb_t("ident", [P, P])
        ident_bf = sb_t("ident_bf", [P, P], BF16)
        ones = sb_t("ones", [P, P])
        zeros_bf = sb_t("zeros_bf", [P, ROWS_PER_SB], BF16)
        w_in = sb_t("w_in", [F, F])
        w_t = sb_t("w_t", [F, F])
        a_in = sb_t("a_in", [F, 2])
        a_rep = sb_t("a_rep", [F, 2, P])
        wa = sb_t("wa", [P, 2, F])
        ent_sum = sb_t("ent_sum", [P, FA])
        diag = sb_t("diag", [P, 2, ROWS_PER_SB])
        v_diag = sb_t("v_diag", [P, 2, ROWS_PER_SB], BF16)
        s_col = sb_t("s_col", [P, RB])
        t_max_part = sb_t("t_max_part", [P, RB, G])
        t_max = sb_t("t_max", [P, RB])
        top = sb_t("top", [P, RB])
        guard = sb_t("guard", [P, RB])
        v_col = sb_t("v_col", [P, RB])
        no_edge = sb_t("no_edge", [P, 3, RB])
        dot_junk = sb_t("dot_junk", [P, RB, F])
        sums = sb_t("sums", [P, RB, FA])
        inv_den = sb_t("inv_den", [P, RB])
        h = sb_t("h", [P, RB, F])
        h_neg = sb_t("h_neg", [P, RB, F])
        y = sb_t("y", [P, RB, F])
        stat = sb_t("stat", [P, 6, RB])
        rstd_guess = sb_t("rstd_guess", [P, RB])
        minus_half = sb_t("minus_half", [P, RB])
        res = sb_t("res", [P, 2, RB, F])

        z_a = ctx.enter_context(nc.psum_tensor("z_a", [P, 2, 2 * ROWS_PER_SB], F32))
        z_d = ctx.enter_context(nc.psum_tensor("z_d", [P, 2, ROWS_PER_SB], F32))
        acc = ctx.enter_context(nc.psum_tensor("acc", [P, 2, 512], F32))

        small_in = sem("small_in")
        ent_in = sem("ent_in")
        x_in = sem("x_in")
        adj_arrived = [sem(f"adj_arrived{r}") for r in range(RB)]
        pool_done = sem("pool_done")
        consts_made = sem("consts_made")
        setup_pe = sem("setup_pe")
        setup_dve = sem("setup_dve")
        setup_self = sem("setup_self")
        t_diag_made = sem("t_diag_made")
        t_spread = sem("t_spread")
        t_row_made = sem("t_row_made")
        ent_summed = sem("ent_summed")
        banks_marked = sem("banks_marked")
        mask_made = sem("mask_made")
        max_made = sem("max_made")
        guard_made = sem("guard_made")
        s_spread = sem("s_spread")
        s_kept = sem("s_kept")
        s_made = sem("s_made")
        s_diag_made = sem("s_diag_made")
        guard_step = sem("guard_step")
        sums_step = sem("sums_step")
        center_step = sem("center_step")
        normalize_step = sem("normalize_step")
        var_made = sem("var_made")
        rstd_guessed = sem("rstd_guessed")
        z_a_written = sem("z_a_written")
        z_d_written = sem("z_d_written")
        z_masked = sem("z_masked")
        probs_made = sem("probs_made")
        probs_used = sem("probs_used")
        acc_done = sem("acc_done")
        acc_taken = sem("acc_taken")
        h_made = sem("h_made")
        elu_made = sem("elu_made")
        res_made = sem("res_made")
        out_done = sem("out_done")
        res_stored = sem("res_stored")

        x_tiles = x.rearrange("(s r p) f -> s p r f", r=RB, p=P)
        out_tiles = out.rearrange("(s r p) f -> s p r f", r=RB, p=P)
        scratch = mask[:, SLOTS - 1].bitcast(F32)
        scratch = scratch.rearrange("p r c -> p (r c)")[:, 0:JT * F].rearrange("p (t f) -> p t f", f=F)
        T_SPREADS = JT // RB

        assert (CYCLE * G) % SLOTS == 0 and CYCLE % X_BUFS == 0 and (SB - 4) % CYCLE == 0
        block = ctx.enter_context(nc.Block())

        def pick(tensor, index):
            names = " ".join("abc"[:len(tensor.shape) - 2])
            return tensor[:, bass.ds(index, 1)].rearrange(f"p o {names} -> p (o {names[0]}) {names[1:]}"
                                                          if names else "p o -> p o")

        def wait_apart(engine, *waits):
            values = [(signal, engine.to_reg(value)) for signal, value in waits]
            engine.wait_ge(pool_done, 3)
            for signal, value in values:
                engine.wait_ge(signal, value)

        @block.sync
        def _(sp):
            sp.dma_start(w_in[:], W).then_inc(small_in, 16)
            for c in range(2):
                sp.dma_start(a_in[:, c:c + 1], a[c * F:(c + 1) * F, :]).then_inc(small_in, 16)
            sp.dma_start(ent_aug[:, :, 0:F], ent.rearrange("(t p) f -> p t f", p=P)).then_inc(ent_in, 16)

            def load_group(s, g, fresh=False):
                n = s * G + g
                for r in range(RB):
                    if not fresh:
                        sp.wait_ge(max_made, n * RB + (r + 1 - RB))
                    sp.dma_start(adj_in[:, r, :],
                                 adj[bass.ds((s * RB + r) * P, P), bass.ds(g * GROUP_COLS, GROUP_COLS)]
                                 ).then_inc(adj_arrived[r], 16)

            def load_x(s):
                sp.dma_start(pick(x_sb, s % X_BUFS), x_tiles[bass.ds(s, 1)].rearrange("o p r f -> p (o r) f")
                             ).then_inc(x_in, 16)

            load_group(0, 0, fresh=True)
            sp.dma_start(x_sb[:, 0], x_tiles[0]).then_inc(x_in, 16)
            with sp.Fori(1, G) as g:
                load_group(0, g)
            with sp.Fori(1, X_BUFS) as s:
                with sp.Fori(0, G) as g:
                    load_group(s, g)
                wait_apart(sp, (x_in, s * 16))
                load_x(s)
            with sp.Fori(X_BUFS, SB) as s:
                with sp.Fori(0, G) as g:
                    load_group(s, g)
                wait_apart(sp, (x_in, s * 16), (res_made, s - (X_BUFS - 1)))
                load_x(s)

        @block.gpsimd
        def _(pool):
            nc.gpsimd.memset(ident[:], 0.0).then_inc(pool_done, 1)
            nc.gpsimd.memset(minus_half[:], -0.5).then_inc(pool_done, 1)
            pool.wait_ge(pool_done, 2)
            nc.gpsimd.affine_select(out=ident[:], in_=ident[:], compare_op=ALU.not_equal, fill=1.0, base=0,
                                    pattern=[[-1, P]], channel_multiplier=1).then_inc(pool_done, 1)
            pool.sem_inc(res_stored, 1)
            with pool.Fori(0, SB) as s:
                pool.wait_ge(var_made, s + 1)
                nc.gpsimd.tensor_tensor(rstd_guess[:], stat[:, 2, :], minus_half[:], ALU.pow
                                        ).then_inc(rstd_guessed, 1)
                pool.wait_ge(res_made, s + 1)
                pool.dma_start(out_tiles[bass.ds(s, 1)].rearrange("o p r f -> p (o r) f"),
                               pick(res, s % 2)).then_inc(out_done, 16)
                pool.wait_ge(out_done, s * 16 + 16)
                pool.sem_inc(res_stored, 1)

        @block.scalar
        def _(act):
            for q in range(T_SPREADS):
                act.wait_ge(t_spread, q + 1)
                nc.scalar.activation(t_row[:, q * ROWS_PER_SB:(q + 1) * ROWS_PER_SB], z_a[:, q % 2, 0:ROWS_PER_SB],
                                     ACT.Copy).then_inc(t_row_made, 1)

            def leaky(s, g, k):
                _, first, nth = ITEMS[k]
                n = s * G + g
                wait_apart(act, (probs_made, n * NI + (NI + item_before("A", nth, 2) + 1)))
                for u in range(2):
                    ins = nc.scalar.activation(z_a[:, nth % 2, u * ROWS_PER_SB:(u + 1) * ROWS_PER_SB],
                                               pick(s_row, s % 2), ACT.Relu,
                                               bias=t_hi[:, bass.ds(g * GT + (first + u), 1)])
                ins.then_inc(z_a_written, 1)

            def exponential(s, g, k):
                kind, first, nth = ITEMS[k]
                n = s * G + g
                wait_apart(act, (z_masked, n * NI + (SLOTS * NI + k + 1)),
                           (probs_used, n * NI + (NI + item_before(kind, nth, 2) + 1)))
                z, probs = (z_a, probs_a) if kind == "A" else (z_d, probs_d)
                for u in range(2 if kind == "A" else 1):
                    cols = slice(u * ROWS_PER_SB, (u + 1) * ROWS_PER_SB)
                    ins = nc.scalar.activation(probs[:, nth % 2, cols], z[:, nth % 2, cols], ACT.Exp,
                                               bias=t_lo[:, bass.ds(g * GT + (first + u), 1)])
                ins.then_inc(probs_made, 1)

            def group(s, g, following=None):
                for k in range(1, NI):
                    if ITEMS[k][0] == "A":
                        leaky(s, g, k)
                    exponential(s, g, k - 1)
                if following is not None:
                    leaky(*following, 0)
                exponential(s, g, NI - 1)

            def elu(s):
                act.wait_ge(h_made, s + 1)
                nc.scalar.activation(h_neg[:], h_neg[:], ACT.Exp).then_inc(elu_made, 1)

            def superblock(s, first=False, last=False):
                group(s, 0, (s, 1))
                if not first:
                    elu(s - 1)
                with act.Fori(1, G - 1) as g:
                    group(s, g, (s, g + 1))
                if last:
                    group(s, G - 1)
                else:
                    for k in range(1, NI):
                        if ITEMS[k][0] == "A":
                            leaky(s, G - 1, k)
                        exponential(s, G - 1, k - 1)
                    act.wait_ge(s_kept, s + 2)
                    leaky(s + 1, 0, 0)
                    exponential(s, G - 1, NI - 1)

            act.sem_inc(probs_made, NI)
            act.wait_ge(banks_marked, 1)
            act.wait_ge(s_kept, 1)
            leaky(0, 0, 0)
            superblock(0, first=True)
            with act.Fori(1, SB - 1) as s:
                superblock(s)
            superblock(SB - 1, last=True)
            elu(SB - 1)

        @block.tensor
        def _(pe):
            pe.wait_ge(small_in, 48)
            pe.wait_ge(consts_made, 1)
            pe.transpose(acc[0:F, 0, 0:F], w_in[:], ident[0:F, 0:F]).then_inc(setup_pe, 1)
            pe.wait_ge(setup_dve, 1)
            for c in range(2):
                mm = pe.matmul(acc[:, 0, c * F:(c + 1) * F], a_rep[:, c, :], w_t[:], start=True, stop=True)
            mm.then_inc(setup_pe, 1)
            pe.wait_ge(setup_dve, 4)
            pe.transpose(acc[0:2, 1, 0:P], t_ends_part[:], ident[:]).then_inc(setup_pe, 1)
            pe.wait_ge(setup_dve, 6)
            pe.matmul(acc[:, 1, 0:2], ones[0:2, :], t_ends_diag[:], start=True, stop=True).then_inc(setup_pe, 1)
            for q in range(T_SPREADS):
                pe.wait_ge(t_diag_made, q + 1)
                if q >= 2:
                    pe.wait_ge(t_row_made, q - 1)
                pe.matmul(z_a[:, q % 2, 0:ROWS_PER_SB], ones[:], diag[:, q % 2, :], start=True, stop=True
                          ).then_inc(t_spread, 1)
            for t in range(JT):
                mm = pe.matmul(acc[:, 0, 0:FA], ones[:], ent_aug[:, t, :], start=(t == 0), stop=(t == JT - 1))
            mm.then_inc(ent_summed, 1)
            pe.wait_ge(t_row_made, T_SPREADS)
            for half in range(2):
                for b in range(2):
                    pe.matmul(z_a[:, half, b * ROWS_PER_SB:(b + 1) * ROWS_PER_SB], zeros_bf[:, 0:P], zeros_bf[:],
                              start=True, stop=True)
                mm = pe.matmul(z_d[:, half, :], zeros_bf[:, 0:P], zeros_bf[:], start=True, stop=True)
            mm.then_inc(banks_marked, 1)

            def add_mask(s, g, k, parity):
                kind, first, nth = ITEMS[k]
                n = s * G + g
                if kind == "A":
                    pe.wait_ge(z_a_written, n * NA + (nth + 1))
                    banks = [z_a[:, nth % 2, 0:ROWS_PER_SB], z_a[:, nth % 2, ROWS_PER_SB:2 * ROWS_PER_SB]]
                else:
                    pe.wait_ge(z_d_written, n * ND + (nth + 1))
                    banks = [z_d[:, nth % 2, :]]
                slot = pick(mask, n % SLOTS)
                for u, z in enumerate(banks):
                    for r in range(RB):
                        mm = pe.matmul(z[:, r * P:(r + 1) * P], slot[:, r, (first + u) * P:(first + u + 1) * P],
                                       v_diag[:, parity, r * P:(r + 1) * P],
                                       start=False, stop=True, skip_group_check=True)
                mm.then_inc(z_masked, 1)

            def weigh(s, g, k, parity):
                kind, first, nth = ITEMS[k]
                n = s * G + g
                pe.wait_ge(probs_made, n * NI + (NI + k + 1))
                for u in range(2 if kind == "A" else 1):
                    for r in range(RB):
                        c = (u * RB + r) * P
                        lhs = probs_a[:, nth % 2, c:c + P] if kind == "A" else probs_d[:, nth % 2, c:c + P]
                        mm = pe.matmul(acc[:, parity, r * FA:(r + 1) * FA], lhs, pick(ent_aug, g * GT + (first + u)),
                                       start=False, stop=True, skip_group_check=True)
                mm.then_inc(probs_used, 1)

            def spread_s(s, parity):
                pe.wait_ge(s_diag_made, s + 1)
                pe.matmul(acc[:, parity, :], ones[:], diag[:, 0, :], start=True, stop=True).then_inc(s_spread, 1)

            def clear_acc(s, parity):
                pe.wait_ge(s_kept, s + 1)
                pe.matmul(acc[:, parity, 0:RB * FA], zeros_bf[:, 0:P], zeros_bf[:, 0:RB * FA], start=True, stop=True)

            def superblock(s, parity, last=False):
                with pe.Fori(0, G - 1) as g:
                    for k in range(1, NI):
                        add_mask(s, g, k, parity)
                        weigh(s, g, k - 1, parity)
                    add_mask(s, g + 1, 0, parity)
                    weigh(s, g, NI - 1, parity)
                for k in range(1, NI):
                    add_mask(s, G - 1, k, parity)
                    weigh(s, G - 1, k - 1, parity)
                    if not last and k == SPREAD_S_AT:
                        spread_s(s + 1, 1 - parity)
                    if not last and k == CLEAR_AT:
                        clear_acc(s + 1, 1 - parity)
                if not last:
                    pe.wait_ge(guard_made, s + 2)
                    add_mask(s + 1, 0, 0, 1 - parity)
                weigh(s, G - 1, NI - 1, parity)

            pe.sem_inc(z_masked, SLOTS * NI)
            pe.sem_inc(probs_used, NI)
            spread_s(0, 0)
            clear_acc(0, 0)
            pe.wait_ge(guard_made, 1)
            add_mask(0, 0, 0, 0)
            superblock(0, 0)
            with pe.Fori(1, SB - 1, 2) as s:
                superblock(s, 1)
                superblock(s + 1, 0)
            superblock(SB - 1, 1, last=True)

        @block.vector
        def _(dve):
            nc.vector.memset(ones[:], 1.0).then_inc(setup_self, 1)
            nc.vector.memset(zeros_bf[:], 0.0).then_inc(setup_self, 1)
            nc.vector.memset(ent_aug[:, :, F:FA], 1.0).then_inc(setup_self, 1)
            dve.wait_ge(pool_done, 3)
            nc.vector.tensor_copy(ident_bf[:], ident[:]).then_inc(setup_self, 1)
            dve.wait_ge(setup_self, 4)
            dve.sem_inc(consts_made, 1)
            dve.wait_ge(small_in, 48)
            for c in range(2):
                nc.vector.tensor_scalar(a_rep[:, c, :], ones[0:F, :], a_in[:, c:c + 1], None, ALU.mult
                                        ).then_inc(setup_self, 1)
            dve.wait_ge(setup_pe, 1)
            dve.wait_ge(setup_self, 6)
            nc.vector.tensor_copy(w_t[:], acc[0:F, 0, 0:F]).then_inc(setup_dve, 1)
            dve.wait_ge(setup_pe, 2)
            nc.vector.tensor_copy(wa[:].rearrange("p c f -> p (c f)"), acc[:, 0, 0:2 * F]).then_inc(setup_dve, 1)
            dve.wait_ge(ent_in, 16)
            dve.wait_ge(setup_dve, 2)
            nc.vector.tensor_tensor(scratch, ent_aug[:, :, 0:F],
                                    wa[:, 1:2, :].broadcast_to([P, JT, F]), ALU.mult).then_inc(setup_dve, 1)
            dve.wait_ge(setup_dve, 3)
            nc.vector.tensor_reduce(t_col[:], scratch, AX_X, ALU.add).then_inc(setup_self, 1)
            dve.wait_ge(setup_self, 7)
            nc.vector.tensor_scalar(t_hi[:], t_col[:], 1.0 - ALPHA, None, ALU.mult)
            nc.vector.tensor_scalar(t_below[:], t_col[:], -1.0, None, ALU.mult).then_inc(setup_self, 1)
            nc.vector.tensor_reduce(t_ends_part[:, 0:1], t_col[:], AX_X, ALU.max)
            dve.wait_ge(setup_self, 8)
            nc.vector.tensor_reduce(t_ends_part[:, 1:2], t_below[:], AX_X, ALU.max).then_inc(setup_dve, 1)
            dve.wait_ge(setup_pe, 3)
            nc.vector.tensor_reduce(t_ends_col[:], acc[0:2, 1, 0:P], AX_X, ALU.max).then_inc(setup_dve, 1)
            dve.wait_ge(setup_dve, 5)
            nc.vector.tensor_scalar(t_ends_diag[:], ident[0:2, 0:2], t_ends_col[:], None, ALU.mult
                                    ).then_inc(setup_dve, 1)
            dve.wait_ge(setup_pe, 4)
            nc.vector.tensor_copy(t_ends[:], acc[:, 1, 0:2]).then_inc(setup_self, 1)
            dve.wait_ge(setup_self, 9)
            nc.vector.tensor_scalar(t_ref[:], t_ends[:, 0:1], 1.0, None, ALU.add)
            nc.vector.tensor_scalar(t_shift[:], t_ends[:, 1:2], ALPHA, 1.0, ALU.mult, ALU.add).then_inc(setup_self, 1)
            dve.wait_ge(setup_self, 10)
            nc.vector.tensor_scalar(t_below[:], t_col[:], t_ref[:], None, ALU.subtract).then_inc(setup_self, 1)
            nc.vector.tensor_scalar(t_lo[:], t_col[:], ALPHA, t_shift[:], ALU.mult, ALU.add)
            nc.vector.tensor_tensor(t_least[:], t_ends[:, 1:2], t_ref[:], ALU.add).then_inc(setup_self, 1)
            dve.wait_ge(setup_self, 12)
            nc.vector.tensor_scalar(t_least[:], t_least[:], -EDGE, None, ALU.mult).then_inc(setup_self, 1)
            for q in range(T_SPREADS):
                if q >= 2:
                    dve.wait_ge(t_spread, q - 1)
                for c in range(RB):
                    ins = nc.vector.tensor_scalar(diag[:, q % 2, c * P:(c + 1) * P], ident[:],
                                                  t_below[:, RB * q + c:RB * q + c + 1], None, ALU.mult)
                ins.then_inc(t_diag_made, 1)
            dve.wait_ge(ent_summed, 1)
            nc.vector.tensor_copy(ent_sum[:], acc[:, 0, 0:FA]).then_inc(setup_self, 1)
            dve.wait_ge(setup_self, 14)
            dve.wait_ge(t_row_made, T_SPREADS)

            def make_mask(s, phase, g, r):
                n = s * G + g
                dve.wait_ge(adj_arrived[r], n * 16 + 16)
                dve.wait_ge(z_masked, n * NI + NI)
                nc.vector.tensor_scalar(mask[:, (phase * G + g) % SLOTS, r, :], adj_in[:, r, :], 0.0, EDGE,
                                        ALU.is_le, ALU.max).then_inc(mask_made, 1)

            def find_max(s, phase, g, r):
                wait_apart(dve, (mask_made, (s * G + g) * RB + (r + 1)))
                spent = adj_in[:, r, :].bitcast(BF16)[:, 0:GROUP_COLS]
                nc.vector.tensor_tensor_reduce(spent, mask[:, (phase * G + g) % SLOTS, r, :],
                                               t_row[:, g * GROUP_COLS:(g + 1) * GROUP_COLS],
                                               1.0, NO_MAX, ALU.mult, ALU.max,
                                               t_max_part[:, r, g:g + 1]).then_inc(max_made, 1)

            def leaky(s, g, nth, fresh=False):
                first = ITEMS[D_AT[nth]][1]
                if not fresh:
                    dve.wait_ge(probs_made, (s * G + g) * NI + (NI + item_before("D", nth, 2) + 1))
                nc.vector.tensor_scalar(z_d[:, nth % 2, :], pick(s_row, s % 2),
                                        t_hi[:, bass.ds(g * GT + first, 1)], 0.0, ALU.add, ALU.max
                                        ).then_inc(z_d_written, 1)

            def chain(signal, rounds_done, steps):
                taken = []

                def then(ins):
                    taken.append(1)
                    assert len(taken) <= steps
                    ins.then_inc(signal, 1)
                    dve.wait_ge(signal, rounds_done * steps + len(taken))

                return then

            def make_s(s, phase):
                wait_apart(dve, (x_in, s * 16 + 16))
                xs = x_sb[:, phase % X_BUFS]
                for r in range(RB):
                    ins = nc.vector.tensor_tensor_reduce(dot_junk[:, r, :], xs[:, r, :], wa[:, 0, :], 1.0, 0.0,
                                                         ALU.mult, ALU.add, s_col[:, r:r + 1])
                ins.then_inc(s_made, 1)
                dve.wait_ge(s_made, s + 1)
                for r in range(RB):
                    ins = nc.vector.tensor_scalar(diag[:, 0, r * P:(r + 1) * P], ident[:], s_col[:, r:r + 1],
                                                  1.0 - ALPHA, ALU.mult, ALU.mult)
                ins.then_inc(s_diag_made, 1)

            def make_guard(s):
                then = chain(guard_step, s, 6)
                dve.wait_ge(max_made, s * (G * RB) + G * RB)
                then(nc.vector.tensor_reduce(t_max[:], t_max_part[:], AX_X, ALU.max))
                nc.vector.tensor_scalar(pick(no_edge, s % 3), t_max[:], -0.5, None, ALU.is_lt)
                then(nc.vector.tensor_scalar(top[:], t_max[:], t_least[:], FROM_EDGE, ALU.max, ALU.mult))
                then(nc.vector.scalar_tensor_tensor(out=top[:], in0=top[:], scalar=t_ref[:], in1=s_col[:],
                                                    op0=ALU.add, op1=ALU.add))
                then(nc.vector.scalar_tensor_tensor(out=guard[:], in0=top[:], scalar=ALPHA, in1=top[:],
                                                    op0=ALU.mult, op1=ALU.max))
                then(nc.vector.scalar_tensor_tensor(out=v_col[:], in0=s_col[:], scalar=ALPHA, in1=guard[:],
                                                    op0=ALU.mult, op1=ALU.subtract))
                then(nc.vector.tensor_scalar(v_col[:], v_col[:], t_shift[:], -1.0, ALU.subtract, ALU.min))
                for r in range(RB):
                    ins = nc.vector.tensor_scalar(pick(v_diag, s % 2)[:, r * P:(r + 1) * P],
                                                  ident_bf[:], v_col[:, r:r + 1], FROM_EDGE, ALU.mult, ALU.mult)
                ins.then_inc(guard_made, 1)

            def keep_s(s):
                dve.wait_ge(s_spread, s + 1)
                nc.vector.tensor_copy(pick(s_row, s % 2), pick(acc, s % 2)).then_inc(s_kept, 1)
                dve.wait_ge(s_kept, s + 1)

            def take_sums(s):
                then = chain(sums_step, s, 2)
                xs = pick(x_sb, s % X_BUFS)
                ne = pick(no_edge, s % 3)
                acc_rb = pick(acc, s % 2)[:, 0:RB * FA].rearrange("p (r f) -> p r f", r=RB)
                dve.wait_ge(probs_used, s * (G * NI) + (G * NI + NI))
                for r in range(RB):
                    ins = nc.vector.scalar_tensor_tensor(out=sums[:, r, :], in0=ent_sum[:], scalar=ne[:, r:r + 1],
                                                         in1=acc_rb[:, r, :], op0=ALU.mult, op1=ALU.add)
                ins.then_inc(acc_taken, 1)
                dve.wait_ge(acc_taken, s + 1)
                then(nc.vector.reciprocal(inv_den[:], sums[:, :, F]))
                for r in range(RB):
                    ins = nc.vector.scalar_tensor_tensor(out=h[:, r, :], in0=sums[:, r, 0:F], scalar=inv_den[:, r:r + 1],
                                                         in1=xs[:, r, :], op0=ALU.mult, op1=ALU.add)
                then(ins)
                nc.vector.tensor_scalar(h_neg[:], h[:], 0.0, None, ALU.min).then_inc(h_made, 1)

            def center(s):
                then = chain(center_step, s, 6)
                xs = pick(x_sb, s % X_BUFS)
                mean, ss = stat[:, 0, :], stat[:, 1, :]
                then(nc.vector.tensor_scalar(y[:], h[:], 0.0, -1.0, ALU.max, ALU.add))
                then(nc.vector.tensor_tensor(y[:], y[:], xs, ALU.add))
                dve.wait_ge(elu_made, s + 1)
                then(nc.vector.tensor_tensor(y[:], y[:], h_neg[:], ALU.add))
                then(nc.vector.tensor_reduce(ss, y[:], AX_X, ALU.add))
                then(nc.vector.tensor_scalar(mean, ss, 1.0 / F, None, ALU.mult))
                for r in range(RB):
                    ins = nc.vector.tensor_scalar(y[:, r, :], y[:, r, :], mean[:, r:r + 1], None, ALU.subtract)
                then(ins)

            def normalize(s):
                then = chain(normalize_step, s, 5)
                ss, var, half, g2, rstd = (stat[:, q, :] for q in range(1, 6))
                for r in range(RB):
                    ins = nc.vector.tensor_tensor_reduce(dot_junk[:, r, :], y[:, r, :], y[:, r, :], 1.0, 0.0,
                                                         ALU.mult, ALU.add, ss[:, r:r + 1])
                then(ins)
                nc.vector.tensor_scalar(var, ss, 1.0 / F, EPS, ALU.mult, ALU.add).then_inc(var_made, 1)
                dve.wait_ge(rstd_guessed, s + 1)
                then(nc.vector.tensor_tensor(g2, rstd_guess[:], rstd_guess[:], ALU.mult))
                then(nc.vector.tensor_tensor(half, g2, var, ALU.mult))
                then(nc.vector.tensor_scalar(half, half, -0.5, 1.5, ALU.mult, ALU.add))
                then(nc.vector.tensor_tensor(rstd, half, rstd_guess[:], ALU.mult))
                dve.wait_ge(res_stored, s + 1)
                for r in range(RB):
                    ins = nc.vector.tensor_scalar(pick(res, s % 2)[:, r, :], y[:, r, :], rstd[:, r:r + 1], None, ALU.mult)
                ins.then_inc(res_made, 1)

            def group(s, g, made, extra, last=False):
                for r in range(RB):
                    if made:
                        make_mask(*made, r)
                    if r < RB - 2:
                        leaky(s, g, r + 2)
                    elif g < G - 1:
                        leaky(s, g + 1, r - (RB - 2))
                    elif not last:
                        leaky(s + 1, 0, r - (RB - 2))
                    if made:
                        find_max(*made, r)
                    for stage in extra.get((g, r), []):
                        stage()

            def superblock(s, phase, first=False, ahead=2):
                following = (phase + 1) % CYCLE
                extra = {}

                def at(g, r, stage):
                    extra.setdefault((g, r), []).append(stage)

                if not first:
                    at(0, 1, lambda: take_sums(s - 1))
                    at(1, 1, lambda: center(s - 1))
                    at(1, 3, lambda: normalize(s - 1))
                if ahead:
                    at(2, 1, lambda: make_s(s + 1, following))
                    at(2, 3, lambda: make_guard(s + 1))
                    at(3, 1, lambda: keep_s(s + 1))
                for g in range(G):
                    if g < G - 1:
                        made = (s + 1, following, g + 1) if ahead else None
                    else:
                        made = (s + 2, (phase + 2) % CYCLE, 0) if ahead > 1 else None
                    if first and g == 0:
                        group(s, g, (s + 1, following, 0), extra)
                        for r in range(RB):
                            make_mask(*made, r)
                            find_max(*made, r)
                    else:
                        group(s, g, made, extra, last=not ahead)

            for g in range(G):
                for r in range(RB):
                    make_mask(0, 0, g, r)
                    find_max(0, 0, g, r)
            make_s(0, 0)
            make_guard(0)
            keep_s(0)
            for nth in range(2):
                leaky(0, 0, nth, fresh=True)
            superblock(0, 0, first=True)
            with dve.Fori(1, SB - 3, CYCLE) as s:
                for c in range(CYCLE):
                    superblock(s + c, (1 + c) % CYCLE)
            superblock(SB - 3, (SB - 3) % CYCLE)
            superblock(SB - 2, (SB - 2) % CYCLE, ahead=1)
            superblock(SB - 1, (SB - 1) % CYCLE, ahead=0)
            take_sums(SB - 1)
            center(SB - 1)
            normalize(SB - 1)


def kernel(**inputs):
    import numpy as _np
    import concourse.bacc as _bacc
    from concourse.bass_utils import run_bass_kernel_spmd as _run

    names = ["x", "adj", "L0_gnn_entity_embs", "L0_gnn_W", "L0_gnn_a"]
    nc = _bacc.Bacc("TRN2", target_bir_lowering=False, num_devices=1)
    arrays, args = {}, []
    for name in names:
        v = _np.ascontiguousarray(inputs[name])
        arrays[f"in_{name}"] = v
        args.append(nc.dram_tensor(f"in_{name}", v.shape, mybir.dt.from_np(v.dtype), kind="ExternalInput").ap())
    out = nc.dram_tensor("out", inputs["x"].shape, F32, kind="ExternalOutput").ap()
    build_gat_layer(nc, *args, out)
    return _run(nc, [arrays], core_ids=[0]).results[0]["out"]
```

```python
from contextlib import ExitStack

import concourse.bass as bass
from concourse import mybir

ALU = mybir.AluOpType
ACT = mybir.ActivationFunctionType
AX_X = mybir.AxisListType.X
F32 = mybir.dt.float32
BF16 = mybir.dt.bfloat16
I32 = mybir.dt.int32

P = 128
ROWS_PER_SB = 512
RB = ROWS_PER_SB // P
GROUP_COLS = 2048
GT = GROUP_COLS // P
SLOTS = 6
EDGE = 2.0 ** -64
FROM_EDGE = 1.0 / EDGE
NO_MAX = -3.0e38
ALPHA = 0.2
EPS = 1e-5
ENT_PARTS = 4
EARLY_BLOCKS = 2
X_BUFS = 4
CYCLE = 3

ORDER = "ADADAADADA"
ITEMS = []
for _kind in ORDER:
    _first = sum(2 if k == "A" else 1 for k, _, _ in ITEMS)
    ITEMS.append((_kind, _first, sum(1 for k, _, _ in ITEMS if k == _kind)))
NI = len(ITEMS)
NA = ORDER.count("A")
ND = ORDER.count("D")
assert 2 * NA + ND == GT and NA % 2 == 0 and ND == RB
A_AT = [i for i, (k, _, _) in enumerate(ITEMS) if k == "A"]
D_AT = [i for i, (k, _, _) in enumerate(ITEMS) if k == "D"]
SPREAD_S_AT = 0
AHEAD = 2
WARM_UP = 16


def item_before(kind, nth, back):
    count = NA if kind == "A" else ND
    wrapped = (nth - back) % count
    where = [i for i, (k, _, q) in enumerate(ITEMS) if k == kind and q == wrapped][0]
    return where + NI * ((nth - back) // count)


def build_gat_layer(nc, x, adj, ent, W, a, out):
    N, M = adj.shape
    F = W.shape[0]
    FA = F + 1
    JT = M // P
    G = M // GROUP_COLS
    SB = N // ROWS_PER_SB
    assert W.shape[1] == F and N == SB * ROWS_PER_SB and M == G * GROUP_COLS

    with ExitStack() as ctx:
        def sb_t(name, shape, dt=F32):
            return ctx.enter_context(nc.sbuf_tensor(name, shape, dt))

        def sem(name):
            return ctx.enter_context(nc.semaphore(name))

        adj_in = sb_t("adj_in", [P, RB, GROUP_COLS], I32)
        mask = sb_t("mask", [P, SLOTS, RB, GROUP_COLS], BF16)
        t_row = sb_t("t_row", [P, M], BF16)
        ent_aug = sb_t("ent_aug", [P, JT, FA])
        probs_a = sb_t("probs_a", [P, 2, 2 * ROWS_PER_SB])
        probs_d = sb_t("probs_d", [P, 2, ROWS_PER_SB])
        s_row = sb_t("s_row", [P, 2, ROWS_PER_SB])
        x_sb = sb_t("x_sb", [P, X_BUFS, RB, F])
        t_col = sb_t("t_col", [P, JT])
        t_hi = sb_t("t_hi", [P, JT])
        t_lo = sb_t("t_lo", [P, JT])
        t_below = sb_t("t_below", [P, JT])
        t_ends_part = sb_t("t_ends_part", [P, 2])
        t_ends_col = sb_t("t_ends_col", [2, 1])
        t_ends_diag = sb_t("t_ends_diag", [2, 2])
        t_ends = sb_t("t_ends", [P, 2])
        t_ref = sb_t("t_ref", [P, 1])
        t_least = sb_t("t_least", [P, 1])
        t_shift = sb_t("t_shift", [P, 1])
        ident = sb_t("ident", [P, P])
        ident_bf = sb_t("ident_bf", [P, P], BF16)
        ones = sb_t("ones", [P, P])
        zeros_bf = sb_t("zeros_bf", [P, ROWS_PER_SB], BF16)
        w_in = sb_t("w_in", [F, F])
        w_t = sb_t("w_t", [F, F])
        a_in = sb_t("a_in", [F, 2])
        a_rep = sb_t("a_rep", [F, 2, P])
        wa = sb_t("wa", [P, 2, F])
        ent_sum = sb_t("ent_sum", [P, FA])
        t_diag = probs_a[:, 1, :].bitcast(BF16).rearrange("p (b c) -> p b c", b=4)
        ones_bf = sb_t("ones_bf", [P, P], BF16)
        s_diag = sb_t("s_diag", [P, ROWS_PER_SB])
        s_hi = sb_t("s_hi", [P, RB])
        acc_turned = sb_t("acc_turned", [FA, ROWS_PER_SB])
        inv_den = sb_t("inv_den", [P, RB])
        v_diag = sb_t("v_diag", [P, 2, ROWS_PER_SB], BF16)
        s_col = sb_t("s_col", [P, RB])
        t_max_part = sb_t("t_max_part", [P, RB, G])
        t_max = sb_t("t_max", [P, RB])
        top = sb_t("top", [P, RB])
        guard = sb_t("guard", [P, RB])
        v_col = sb_t("v_col", [P, RB])
        no_edge = sb_t("no_edge", [P, 3, RB])
        sums = sb_t("sums", [P, RB, FA])
        h = sb_t("h", [P, RB, F])
        h_neg = sb_t("h_neg", [P, RB, F])
        y = sb_t("y", [P, RB, F])
        square = sb_t("square", [P, RB, F])
        halves = sb_t("halves", [P, RB, F // 2])
        stat = sb_t("stat", [P, 4, RB])
        minus_half = sb_t("minus_half", [P, RB])
        res = sb_t("res", [P, RB, F])

        z_a = ctx.enter_context(nc.psum_tensor("z_a", [P, 2, 2 * ROWS_PER_SB], F32))
        z_d = ctx.enter_context(nc.psum_tensor("z_d", [P, 2, ROWS_PER_SB], F32))
        acc = ctx.enter_context(nc.psum_tensor("acc", [P, 2, 512], F32))

        small_in = sem("small_in")
        ent_in = [sem(f"ent_in{part}") for part in range(ENT_PARTS)]
        x_in = sem("x_in")
        adj_arrived = [sem(f"adj_arrived{r}") for r in range(RB)]
        pool_done = sem("pool_done")
        consts_made = sem("consts_made")
        setup_pe = sem("setup_pe")
        setup_dve = sem("setup_dve")
        setup_self = sem("setup_self")
        t_diag_made = [sem("t_diag_made_act"), sem("t_diag_made_pool")]
        tables_loaded = sem("tables_loaded")
        t_spread = sem("t_spread")
        t_row_made = sem("t_row_made")
        ent_summed = sem("ent_summed")
        ent_kept = sem("ent_kept")
        banks_marked = sem("banks_marked")
        mask_made = sem("mask_made")
        max_made = sem("max_made")
        guard_made = sem("guard_made")
        s_spread = sem("s_spread")
        s_kept = sem("s_kept")
        s_diag_made = sem("s_diag_made")
        guard_step = sem("guard_step")
        finish_step = sem("finish_step")
        finish_last_step = sem("finish_last_step")
        last_var_made = sem("last_var_made")
        last_rstd_guessed = sem("last_rstd_guessed")
        z_a_written = sem("z_a_written")
        z_d_written = sem("z_d_written")
        z_masked = sem("z_masked")
        probs_made = sem("probs_made")
        probs_used = sem("probs_used")
        acc_kept = sem("acc_kept")
        sums_turned = sem("sums_turned")
        acc_taken = sem("acc_taken")
        h_made = sem("h_made")
        sums_made = sem("sums_made")
        sums_used = sem("sums_used")
        s_step = sem("s_step")
        h_step = sem("h_step")
        wa_made = sem("wa_made")
        t_below_made = sem("t_below_made")
        elu_made = sem("elu_made")
        res_made = sem("res_made")
        out_done = sem("out_done")

        x_tiles = x.rearrange("(s r p) f -> s p r f", r=RB, p=P)
        out_tiles = out.rearrange("(s r p) f -> s p r f", r=RB, p=P)
        scratch = mask[:, SLOTS - 1].bitcast(F32)
        scratch = scratch.rearrange("p r c -> p (r c)")[:, 0:JT * F].rearrange("p (t f) -> p t f", f=F)
        T_SPREADS = JT // RB

        assert (CYCLE * G) % SLOTS == 0 and (SB - 4) % CYCLE == 0
        block = ctx.enter_context(nc.Block())

        def pick(tensor, index):
            names = " ".join("abc"[:len(tensor.shape) - 2])
            return tensor[:, bass.ds(index, 1)].rearrange(f"p o {names} -> p (o {names[0]}) {names[1:]}"
                                                          if names else "p o -> p o")

        def stretch(columns, width):
            return columns.rearrange("p (r o) -> p r o", o=1).broadcast_to([P, RB, width])

        def spread_diag(engine, to, identity, columns):
            return engine.tensor_tensor(to.rearrange("p (r c) -> p r c", r=RB),
                                        identity[:].rearrange("p (o c) -> p o c", o=1).broadcast_to([P, RB, P]),
                                        stretch(columns, P), ALU.mult)

        def wait_apart(engine, *waits):
            values = [(signal, engine.to_reg(value)) for signal, value in waits]
            engine.wait_ge(pool_done, 3)
            for signal, value in values:
                engine.wait_ge(signal, value)

        @block.sync
        def _(sp):
            sp.dma_start(w_in[:], W).then_inc(small_in, 16)
            for c in range(2):
                sp.dma_start(a_in[:, c:c + 1], a[c * F:(c + 1) * F, :]).then_inc(small_in, 16)
            for part in range(ENT_PARTS):
                tiles = slice(part * JT // ENT_PARTS, (part + 1) * JT // ENT_PARTS)
                sp.dma_start(ent_aug[:, tiles, 0:F],
                             ent.rearrange("(t p) f -> p t f", p=P)[:, tiles]).then_inc(ent_in[part], 16)

            def load_group(s, g, free=None):
                n = s * G + g
                for r in range(RB):
                    if free is not None:
                        sp.wait_ge(free, n * RB + (r + 1 - RB))
                    sp.dma_start(adj_in[:, r, :],
                                 adj[bass.ds((s * RB + r) * P, P), bass.ds(g * GROUP_COLS, GROUP_COLS)]
                                 ).then_inc(adj_arrived[r], 16)

            def load_x(s):
                sp.dma_start(pick(x_sb, s % X_BUFS), x_tiles[bass.ds(s, 1)].rearrange("o p r f -> p (o r) f")
                             ).then_inc(x_in, 16)

            load_group(0, 0)
            sp.dma_start(x_sb[:, 0], x_tiles[0]).then_inc(x_in, 16)
            with sp.Fori(1, G) as g:
                load_group(0, g, free=mask_made)
            load_group(1, 0, free=mask_made)
            sp.wait_ge(x_in, 16)
            sp.dma_start(x_sb[:, 1], x_tiles[1]).then_inc(x_in, 16)
            with sp.Fori(1, G) as g:
                load_group(1, g, free=max_made)
            for s in range(2, X_BUFS):
                sp.wait_ge(x_in, s * 16)
                sp.dma_start(x_sb[:, s], x_tiles[s]).then_inc(x_in, 16)
                with sp.Fori(0, G) as g:
                    load_group(s, g, free=max_made)
            with sp.Fori(X_BUFS, SB) as s:
                wait_apart(sp, (x_in, s * 16), (res_made, s - (X_BUFS - 1)))
                load_x(s)
                with sp.Fori(0, G) as g:
                    load_group(s, g, free=max_made)

        @block.gpsimd
        def _(pool):
            nc.gpsimd.memset(ident[:], 0.0).then_inc(pool_done, 1)
            nc.gpsimd.memset(minus_half[:], -0.5).then_inc(pool_done, 1)
            pool.wait_ge(pool_done, 2)
            nc.gpsimd.affine_select(out=ident[:], in_=ident[:], compare_op=ALU.not_equal, fill=1.0, base=0,
                                    pattern=[[-1, P]], channel_multiplier=1).then_inc(pool_done, 1)

            def chain(signal, rounds_done, steps):
                taken = []

                def then(ins):
                    taken.append(1)
                    assert len(taken) <= steps
                    ins.then_inc(signal, 1)
                    wait_apart(pool, (signal, rounds_done * steps + len(taken)))

                return then

            def add_up(then, source):
                width = F // 2
                while width >= 1:
                    then(nc.gpsimd.tensor_tensor(halves[:, :, 0:width], source[:, :, 0:width],
                                                 source[:, :, width:2 * width], ALU.add))
                    source, width = halves, width // 2

            def make_s(s):
                then = chain(s_step, s, 8)
                wait_apart(pool, (x_in, s * 16 + 16), (guard_made, s + 1), (s_spread, s + 1))
                then(nc.gpsimd.tensor_tensor(square[:], pick(x_sb, s % X_BUFS), wa[:, 0:1, :].broadcast_to([P, RB, F]),
                                             ALU.mult))
                add_up(then, square)
                nc.gpsimd.tensor_scalar(s_col[:], halves[:, :, 0], 1.0, None, ALU.mult)
                then(nc.gpsimd.tensor_scalar(s_hi[:], halves[:, :, 0], 1.0 - ALPHA, None, ALU.mult))
                spread_diag(nc.gpsimd, s_diag[:], ident, s_hi[:]).then_inc(s_diag_made, 1)

            def make_h(s):
                then = chain(h_step, s, 2)
                wait_apart(pool, (sums_made, s + 1))
                then(nc.gpsimd.tensor_tensor(h[:], sums[:, :, 0:F], stretch(inv_den[:], F), ALU.mult))
                pool.sem_inc(sums_used, 1)
                then(nc.gpsimd.tensor_tensor(h[:], h[:], pick(x_sb, s % X_BUFS), ALU.add))
                nc.gpsimd.tensor_scalar(h_neg[:], h[:], 0.0, None, ALU.min).then_inc(h_made, 1)

            def finish(s):
                then = chain(finish_step, s, 24)
                mean, var, half, rstd = (stat[:, q, :] for q in range(4))
                then(nc.gpsimd.tensor_scalar(y[:], h[:], 0.0, -1.0, ALU.max, ALU.add))
                then(nc.gpsimd.tensor_tensor(y[:], y[:], pick(x_sb, s % X_BUFS), ALU.add))
                pool.wait_ge(elu_made, s + 1)
                then(nc.gpsimd.tensor_tensor(y[:], y[:], h_neg[:], ALU.add))
                add_up(then, y)
                then(nc.gpsimd.tensor_scalar(mean, halves[:, :, 0], 1.0 / F, None, ALU.mult))
                then(nc.gpsimd.tensor_tensor(y[:], y[:], stretch(mean, F), ALU.subtract))
                then(nc.gpsimd.tensor_tensor(square[:], y[:], y[:], ALU.mult))
                add_up(then, square)
                then(nc.gpsimd.tensor_scalar(var, halves[:, :, 0], 1.0 / F, EPS, ALU.mult, ALU.add))
                then(nc.gpsimd.tensor_tensor(rstd, var, minus_half[:], ALU.pow))
                then(nc.gpsimd.tensor_tensor(half, rstd, rstd, ALU.mult))
                then(nc.gpsimd.tensor_tensor(half, half, var, ALU.mult))
                then(nc.gpsimd.tensor_scalar(half, half, -0.5, 1.5, ALU.mult, ALU.add))
                then(nc.gpsimd.tensor_tensor(rstd, half, rstd, ALU.mult))
                nc.gpsimd.tensor_tensor(res[:], y[:], stretch(rstd, F), ALU.mult).then_inc(res_made, 1)
                pool.wait_ge(res_made, s + 1)
                pool.dma_start(out_tiles[bass.ds(s, 1)].rearrange("o p r f -> p (o r) f"),
                               res[:]).then_inc(out_done, 16)
                pool.wait_ge(out_done, s * 16 + 16)

            pool.sem_inc(guard_made, 1)
            pool.sem_inc(s_spread, 1)
            pool.sem_inc(sums_used, 1)
            pool.wait_ge(wa_made, 1)
            pool.wait_ge(t_below_made, 1)
            for q in range(1, T_SPREADS, 2):
                if q >= 4:
                    pool.wait_ge(t_spread, q - 3)
                spread_diag(nc.gpsimd, t_diag[:, q % 4, :], ident_bf, t_below[:, RB * q:RB * q + RB]
                            ).then_inc(t_diag_made[1], 1)
            make_s(0)
            make_s(1)
            with pool.Fori(0, SB - 2) as s:
                make_h(s)
                make_s(s + 2)
                finish(s)
            make_h(SB - 2)
            finish(SB - 2)
            pool.wait_ge(last_var_made, 1)
            nc.gpsimd.tensor_tensor(stat[:, 3, :], stat[:, 1, :], minus_half[:], ALU.pow
                                    ).then_inc(last_rstd_guessed, 1)
            pool.wait_ge(res_made, SB)
            pool.dma_start(out_tiles[SB - 1], res[:]).then_inc(out_done, 16)
            pool.wait_ge(out_done, SB * 16)

        @block.scalar
        def _(act):
            def make_t_diag(q):
                if q >= 4:
                    act.wait_ge(t_spread, q - 3)
                for c in range(RB):
                    ins = nc.scalar.activation(t_diag[:, q % 4, c * P:(c + 1) * P], ident_bf[:], ACT.Copy,
                                               scale=t_below[:, RB * q + c:RB * q + c + 1])
                ins.then_inc(t_diag_made[0], 1)

            act.wait_ge(consts_made, 1)
            nc.scalar.activation(t_diag[:, 0, 0:P], ident_bf[:], ACT.Exp).then_inc(tables_loaded, 1)
            act.wait_ge(tables_loaded, 1)
            act.wait_ge(t_below_made, 1)
            make_t_diag(0)
            for q in range(T_SPREADS):
                if q % 2 == 0 and q + 2 < T_SPREADS:
                    make_t_diag(q + 2)
                act.wait_ge(t_spread, q + 1)
                nc.scalar.activation(t_row[:, q * ROWS_PER_SB:(q + 1) * ROWS_PER_SB], z_a[:, q % 2, 0:ROWS_PER_SB],
                                     ACT.Copy).then_inc(t_row_made, 1)

            def leaky(s, g, k):
                _, first, nth = ITEMS[k]
                n = s * G + g
                wait_apart(act, (probs_made, n * NI + (NI + item_before("A", nth, 2) + 1)))
                for u in range(2):
                    ins = nc.scalar.activation(z_a[:, nth % 2, u * ROWS_PER_SB:(u + 1) * ROWS_PER_SB],
                                               pick(s_row, s % 2), ACT.Relu,
                                               bias=t_hi[:, bass.ds(g * GT + (first + u), 1)])
                ins.then_inc(z_a_written, 1)

            def exponential(s, g, k):
                kind, first, nth = ITEMS[k]
                n = s * G + g
                wait_apart(act, (z_masked, n * NI + (SLOTS * NI + k + 1)),
                           (probs_used, n * NI + (NI + item_before(kind, nth, 2) + 1)))
                z, probs = (z_a, probs_a) if kind == "A" else (z_d, probs_d)
                for u in range(2 if kind == "A" else 1):
                    cols = slice(u * ROWS_PER_SB, (u + 1) * ROWS_PER_SB)
                    ins = nc.scalar.activation(probs[:, nth % 2, cols], z[:, nth % 2, cols], ACT.Exp,
                                               bias=t_lo[:, bass.ds(g * GT + (first + u), 1)])
                ins.then_inc(probs_made, 1)

            def group(s, g, following=None, next_rows=False):
                for k in range(NI):
                    if ITEMS[k][0] == "A":
                        nxt = [i for i in A_AT if i > k]
                        if nxt:
                            leaky(s, g, nxt[0])
                        elif following is not None:
                            if next_rows:
                                act.wait_ge(s_kept, s + 2)
                            leaky(*following, 0)
                    exponential(s, g, k)

            def elu(s):
                act.wait_ge(h_made, s + 1)
                nc.scalar.activation(h_neg[:], h_neg[:], ACT.Exp).then_inc(elu_made, 1)

            def superblock(s, first=False, last=False):
                with act.Fori(0, G - 1) as g:
                    group(s, g, (s, g + 1))
                if not first:
                    elu(s - 1)
                if last:
                    group(s, G - 1)
                else:
                    group(s, G - 1, (s + 1, 0), next_rows=True)

            act.sem_inc(probs_made, NI)
            act.wait_ge(banks_marked, 1)
            act.wait_ge(s_kept, 1)
            leaky(0, 0, 0)
            superblock(0, first=True)
            with act.Fori(1, SB - 1) as s:
                superblock(s)
            superblock(SB - 1, last=True)
            elu(SB - 1)

        @block.tensor
        def _(pe):
            pe.wait_ge(small_in, 48)
            pe.wait_ge(consts_made, 1)
            pe.transpose(acc[0:F, 0, 0:F], w_in[:], ident[0:F, 0:F]).then_inc(setup_pe, 1)
            pe.wait_ge(setup_dve, 1)
            for c in range(2):
                mm = pe.matmul(acc[:, 0, c * F:(c + 1) * F], a_rep[:, c, :], w_t[:], start=True, stop=True)
            mm.then_inc(setup_pe, 1)
            pe.wait_ge(setup_dve, 3 + ENT_PARTS)
            pe.transpose(acc[0:2, 1, 0:P], t_ends_part[:], ident[:]).then_inc(setup_pe, 1)
            pe.wait_ge(setup_dve, 5 + ENT_PARTS)
            pe.matmul(acc[:, 1, 0:2], ones[0:2, :], t_ends_diag[:], start=True, stop=True).then_inc(setup_pe, 1)
            for q in range(T_SPREADS):
                pe.wait_ge(t_diag_made[q % 2], q // 2 + 1)
                if q >= 2:
                    pe.wait_ge(t_row_made, q - 1)
                pe.matmul(z_a[:, q % 2, 0:ROWS_PER_SB], ones_bf[:], t_diag[:, q % 4, :], start=True, stop=True
                          ).then_inc(t_spread, 1)
            for t in range(JT):
                mm = pe.matmul(acc[:, 0, 0:FA], ones[:], ent_aug[:, t, :], start=(t == 0), stop=(t == JT - 1))
            mm.then_inc(ent_summed, 1)
            pe.wait_ge(t_row_made, T_SPREADS)
            for half in range(2):
                for b in range(2):
                    pe.matmul(z_a[:, half, b * ROWS_PER_SB:(b + 1) * ROWS_PER_SB], zeros_bf[:, 0:P], zeros_bf[:],
                              start=True, stop=True)
                mm = pe.matmul(z_d[:, half, :], zeros_bf[:, 0:P], zeros_bf[:], start=True, stop=True)
            mm.then_inc(banks_marked, 1)

            def add_mask(s, g, k, parity):
                kind, first, nth = ITEMS[k]
                n = s * G + g
                if kind == "A":
                    pe.wait_ge(z_a_written, n * NA + (nth + 1))
                    banks = [z_a[:, nth % 2, 0:ROWS_PER_SB], z_a[:, nth % 2, ROWS_PER_SB:2 * ROWS_PER_SB]]
                else:
                    pe.wait_ge(z_d_written, n * ND + (nth + 1))
                    banks = [z_d[:, nth % 2, :]]
                slot = pick(mask, n % SLOTS)
                for u, z in enumerate(banks):
                    for r in range(RB):
                        mm = pe.matmul(z[:, r * P:(r + 1) * P], slot[:, r, (first + u) * P:(first + u + 1) * P],
                                       v_diag[:, parity, r * P:(r + 1) * P],
                                       start=False, stop=True, skip_group_check=True)
                mm.then_inc(z_masked, 1)

            def weigh(s, g, k, parity):
                kind, first, nth = ITEMS[k]
                n = s * G + g
                if (g, k) == (0, 0):
                    pe.wait_ge(s_kept, s + 1)
                pe.wait_ge(probs_made, n * NI + (NI + k + 1))
                probs = probs_a if kind == "A" else probs_d
                for u in range(2 if kind == "A" else 1):
                    mm = pe.matmul(acc[0:FA, parity, :], ent_aug[:, g * GT + first + u, :],
                                   probs[:, nth % 2, u * ROWS_PER_SB:(u + 1) * ROWS_PER_SB],
                                   start=(g, k, u) == (0, 0, 0), stop=True, skip_group_check=True)
                mm.then_inc(probs_used, 1)

            def spread_s(s, parity, fresh=False):
                pe.wait_ge(s_diag_made, s + 1)
                if not fresh:
                    pe.wait_ge(acc_taken, s - 1)
                pe.matmul(acc[:, parity, :], ones[:], s_diag[:], start=True, stop=True).then_inc(s_spread, 1)

            def turn_sums(s, parity):
                pe.wait_ge(acc_kept, s + 1)
                for r in range(RB):
                    mm = pe.transpose(acc[:, parity, r * FA:(r + 1) * FA], acc_turned[:, r * P:(r + 1) * P],
                                      ident[0:FA, 0:FA])
                mm.then_inc(sums_turned, 1)

            def superblock(s, parity, first=False, last=False):
                for g in range(G):
                    for k in range(NI):
                        if k + AHEAD < NI:
                            add_mask(s, g, k + AHEAD, parity)
                        elif g < G - 1:
                            add_mask(s, g + 1, k + AHEAD - NI, parity)
                        elif not last:
                            if k + AHEAD == NI:
                                pe.wait_ge(guard_made, s + 3)
                            add_mask(s + 1, 0, k + AHEAD - NI, 1 - parity)
                        weigh(s, g, k, parity)
                        if (g, k) == (0, NI - 1) and not first:
                            turn_sums(s - 1, 1 - parity)
                        if (g, k) == (G - 1, SPREAD_S_AT) and not last:
                            spread_s(s + 1, 1 - parity)

            pe.sem_inc(z_masked, SLOTS * NI)
            pe.sem_inc(probs_used, NI)
            pe.wait_ge(ent_kept, 1)
            spread_s(0, 0, fresh=True)
            pe.wait_ge(s_kept, 1)
            pe.wait_ge(max_made, G * RB - 2)
            for _ in range(WARM_UP):
                pe.matmul(acc[:, 0, :], zeros_bf[:, 0:P], zeros_bf[:], start=True, stop=True)
            pe.wait_ge(guard_made, 2)
            for k in range(AHEAD):
                add_mask(0, 0, k, 0)
            superblock(0, 0, first=True)
            with pe.Fori(1, SB - 1, 2) as s:
                superblock(s, 1)
                superblock(s + 1, 0)
            superblock(SB - 1, 1, last=True)
            turn_sums(SB - 1, 1)

        @block.vector
        def _(dve):
            nc.vector.memset(ones[:], 1.0).then_inc(setup_self, 1)
            nc.vector.memset(ones_bf[:], 1.0)
            nc.vector.memset(zeros_bf[:], 0.0).then_inc(setup_self, 1)
            nc.vector.memset(ent_aug[:, :, F:FA], 1.0).then_inc(setup_self, 1)
            dve.wait_ge(pool_done, 3)
            nc.vector.tensor_copy(ident_bf[:], ident[:]).then_inc(setup_self, 1)
            dve.wait_ge(setup_self, 4)
            dve.sem_inc(consts_made, 1)
            dve.wait_ge(small_in, 48)
            for c in range(2):
                nc.vector.tensor_scalar(a_rep[:, c, :], ones[0:F, :], a_in[:, c:c + 1], None, ALU.mult
                                        ).then_inc(setup_self, 1)
            dve.wait_ge(setup_pe, 1)
            dve.wait_ge(setup_self, 6)
            nc.vector.tensor_copy(w_t[:], acc[0:F, 0, 0:F]).then_inc(setup_dve, 1)
            dve.wait_ge(setup_pe, 2)
            nc.vector.tensor_copy(wa[:].rearrange("p c f -> p (c f)"), acc[:, 0, 0:2 * F]).then_inc(setup_dve, 1)
            dve.wait_ge(setup_dve, 2)
            dve.sem_inc(wa_made, 1)
            for part in range(ENT_PARTS):
                tiles = slice(part * JT // ENT_PARTS, (part + 1) * JT // ENT_PARTS)
                dve.wait_ge(ent_in[part], 16)
                nc.vector.tensor_tensor(scratch[:, tiles], ent_aug[:, tiles, 0:F],
                                        wa[:, 1:2, :].broadcast_to([P, JT // ENT_PARTS, F]), ALU.mult).then_inc(setup_dve, 1)
                dve.wait_ge(setup_dve, 3 + part)
                ins = nc.vector.tensor_reduce(t_col[:, tiles], scratch[:, tiles], AX_X, ALU.add)
            ins.then_inc(setup_self, 1)
            dve.wait_ge(setup_self, 7)
            nc.vector.tensor_scalar(t_hi[:], t_col[:], 1.0 - ALPHA, None, ALU.mult)
            nc.vector.tensor_scalar(t_below[:], t_col[:], -1.0, None, ALU.mult).then_inc(setup_self, 1)
            nc.vector.tensor_reduce(t_ends_part[:, 0:1], t_col[:], AX_X, ALU.max)
            dve.wait_ge(setup_self, 8)
            nc.vector.tensor_reduce(t_ends_part[:, 1:2], t_below[:], AX_X, ALU.max).then_inc(setup_dve, 1)
            dve.wait_ge(setup_pe, 3)
            nc.vector.tensor_reduce(t_ends_col[:], acc[0:2, 1, 0:P], AX_X, ALU.max).then_inc(setup_dve, 1)
            dve.wait_ge(setup_dve, 4 + ENT_PARTS)
            nc.vector.tensor_scalar(t_ends_diag[:], ident[0:2, 0:2], t_ends_col[:], None, ALU.mult
                                    ).then_inc(setup_dve, 1)
            dve.wait_ge(setup_pe, 4)
            nc.vector.tensor_copy(t_ends[:], acc[:, 1, 0:2]).then_inc(setup_self, 1)
            dve.wait_ge(setup_self, 9)
            nc.vector.tensor_scalar(t_ref[:], t_ends[:, 0:1], 1.0, None, ALU.add)
            nc.vector.tensor_scalar(t_shift[:], t_ends[:, 1:2], ALPHA, 1.0, ALU.mult, ALU.add).then_inc(setup_self, 1)
            dve.wait_ge(setup_self, 10)
            nc.vector.tensor_scalar(t_below[:], t_col[:], t_ref[:], None, ALU.subtract).then_inc(t_below_made, 1)
            nc.vector.tensor_scalar(t_lo[:], t_col[:], ALPHA, t_shift[:], ALU.mult, ALU.add)
            nc.vector.tensor_tensor(t_least[:], t_ends[:, 1:2], t_ref[:], ALU.add).then_inc(setup_self, 1)
            dve.wait_ge(setup_self, 11)
            nc.vector.tensor_scalar(t_least[:], t_least[:], -EDGE, None, ALU.mult).then_inc(setup_self, 1)
            dve.wait_ge(setup_self, 12)

            def make_mask(s, phase, g, r, fresh=False):
                n = s * G + g
                dve.wait_ge(adj_arrived[r], n * 16 + 16)
                if not fresh:
                    dve.wait_ge(z_masked, n * NI + NI)
                nc.vector.tensor_scalar(mask[:, (phase * G + g) % SLOTS, r, :], adj_in[:, r, :], 0.0, EDGE,
                                        ALU.is_le, ALU.max).then_inc(mask_made, 1)

            def find_max(s, phase, g, r, fresh=False):
                wait_apart(dve, (mask_made, (s * G + g) * RB + (r + 1)))
                spent = adj_in[:, r, :]
                if fresh:
                    spent = probs_a[:, 0, :] if r % 2 == 0 else probs_d[:].rearrange("p b c -> p (b c)")
                    if g * RB + r >= 2:
                        dve.wait_ge(max_made, g * RB + r - 1)
                spent = spent.bitcast(BF16)[:, 0:GROUP_COLS]
                nc.vector.tensor_tensor_reduce(spent, mask[:, (phase * G + g) % SLOTS, r, :],
                                               t_row[:, g * GROUP_COLS:(g + 1) * GROUP_COLS],
                                               1.0, NO_MAX, ALU.mult, ALU.max,
                                               t_max_part[:, r, g:g + 1]).then_inc(max_made, 1)

            def leaky(s, g, nth, fresh=False):
                first = ITEMS[D_AT[nth]][1]
                if not fresh:
                    dve.wait_ge(probs_made, (s * G + g) * NI + (NI + item_before("D", nth, 2) + 1))
                nc.vector.tensor_scalar(z_d[:, nth % 2, :], pick(s_row, s % 2),
                                        t_hi[:, bass.ds(g * GT + first, 1)], 0.0, ALU.add, ALU.max
                                        ).then_inc(z_d_written, 1)

            def chain(signal, rounds_done, steps):
                taken = []

                def then(ins):
                    taken.append(1)
                    assert len(taken) <= steps
                    ins.then_inc(signal, 1)
                    dve.wait_ge(signal, rounds_done * steps + len(taken))

                return then

            def make_guard(s):
                then = chain(guard_step, s, 6)
                dve.wait_ge(max_made, s * (G * RB) + G * RB)
                dve.wait_ge(s_diag_made, s + 1)
                then(nc.vector.tensor_reduce(t_max[:], t_max_part[:], AX_X, ALU.max))
                nc.vector.tensor_scalar(pick(no_edge, s % 3), t_max[:], -0.5, None, ALU.is_lt)
                then(nc.vector.tensor_scalar(top[:], t_max[:], t_least[:], FROM_EDGE, ALU.max, ALU.mult))
                then(nc.vector.scalar_tensor_tensor(out=top[:], in0=top[:], scalar=t_ref[:], in1=s_col[:],
                                                    op0=ALU.add, op1=ALU.add))
                then(nc.vector.scalar_tensor_tensor(out=guard[:], in0=top[:], scalar=ALPHA, in1=top[:],
                                                    op0=ALU.mult, op1=ALU.max))
                then(nc.vector.scalar_tensor_tensor(out=v_col[:], in0=s_col[:], scalar=ALPHA, in1=guard[:],
                                                    op0=ALU.mult, op1=ALU.subtract))
                then(nc.vector.tensor_scalar(v_col[:], v_col[:], t_shift[:], -1.0, ALU.subtract, ALU.min))
                for r in range(RB):
                    ins = nc.vector.tensor_scalar(pick(v_diag, s % 2)[:, r * P:(r + 1) * P],
                                                  ident_bf[:], v_col[:, r:r + 1], FROM_EDGE, ALU.mult, ALU.mult)
                ins.then_inc(guard_made, 1)

            def keep_s(s):
                dve.wait_ge(s_spread, s + 2)
                nc.vector.tensor_copy(pick(s_row, s % 2), pick(acc, s % 2)).then_inc(s_kept, 1)
                dve.wait_ge(s_kept, s + 1)

            def keep_acc(s):
                wait_apart(dve, (probs_used, s * (G * NI) + (G * NI + NI)))
                nc.vector.tensor_copy(acc_turned[:], pick(acc, s % 2)[0:FA]).then_inc(acc_kept, 1)

            def take_sums(s):
                ne = pick(no_edge, s % 3)
                acc_rb = pick(acc, s % 2)[:, 0:RB * FA].rearrange("p (r f) -> p r f", r=RB)
                dve.wait_ge(sums_turned, s + 1)
                dve.wait_ge(sums_used, s + 1)
                for r in range(RB):
                    ins = nc.vector.scalar_tensor_tensor(out=sums[:, r, :], in0=ent_sum[:], scalar=ne[:, r:r + 1],
                                                         in1=acc_rb[:, r, :], op0=ALU.mult, op1=ALU.add)
                ins.then_inc(acc_taken, 1)
                dve.wait_ge(acc_taken, s + 1)
                nc.vector.reciprocal(inv_den[:], sums[:, :, F]).then_inc(sums_made, 1)

            def superblock(s, phase, first=False, ahead=2):
                def blocks_of(later, start, end):
                    return [(s + later, (phase + later) % CYCLE, b // RB, b % RB) for b in range(start, end)]

                blocks = []
                if ahead:
                    blocks += blocks_of(1, 0 if first else EARLY_BLOCKS, G * RB)
                if ahead > 1:
                    blocks += blocks_of(2, 0, EARLY_BLOCKS)
                for g in range(G):
                    for r in range(RB):
                        made = blocks.pop(0) if blocks else None
                        if made:
                            make_mask(*made)
                        if r < RB - 2:
                            leaky(s, g, r + 2)
                        elif g < G - 1:
                            leaky(s, g + 1, r - (RB - 2))
                        elif ahead:
                            leaky(s + 1, 0, r - (RB - 2))
                        if made:
                            find_max(*made)
                        if (g, r) == (0, 1) and not first:
                            keep_acc(s - 1)
                        if (g, r) == (1, 1) and not first:
                            take_sums(s - 1)
                        if (g, r) == (G - 1, 0) and ahead:
                            keep_s(s + 1)
                        if (g, r) == (G - 1, RB - 1 - EARLY_BLOCKS) and ahead:
                            make_guard(s + 1)
                    if first and g < EARLY_BLOCKS:
                        made = blocks.pop(0)
                        make_mask(*made)
                        find_max(*made)

            def finish_last(s):
                taken = []

                def then(ins):
                    taken.append(1)
                    ins.then_inc(finish_last_step, 1)
                    dve.wait_ge(finish_last_step, len(taken))

                xs = x_sb[:, s % X_BUFS]
                mean, var, half, rstd = (stat[:, q, :] for q in range(4))
                dve.wait_ge(sums_made, s + 1)
                dve.wait_ge(res_made, s)
                then(nc.vector.tensor_tensor(h[:], sums[:, :, 0:F], stretch(inv_den[:], F), ALU.mult))
                then(nc.vector.tensor_tensor(h[:], h[:], xs, ALU.add))
                nc.vector.tensor_scalar(h_neg[:], h[:], 0.0, None, ALU.min).then_inc(h_made, 1)
                then(nc.vector.tensor_scalar(y[:], h[:], 0.0, -1.0, ALU.max, ALU.add))
                then(nc.vector.tensor_tensor(y[:], y[:], xs, ALU.add))
                dve.wait_ge(elu_made, s + 1)
                then(nc.vector.tensor_tensor(y[:], y[:], h_neg[:], ALU.add))
                then(nc.vector.tensor_reduce(mean, y[:], AX_X, ALU.add))
                then(nc.vector.tensor_scalar(mean, mean, 1.0 / F, None, ALU.mult))
                then(nc.vector.tensor_tensor(y[:], y[:], stretch(mean, F), ALU.subtract))
                then(nc.vector.tensor_tensor(square[:], y[:], y[:], ALU.mult))
                then(nc.vector.tensor_reduce(var, square[:], AX_X, ALU.add))
                nc.vector.tensor_scalar(var, var, 1.0 / F, EPS, ALU.mult, ALU.add).then_inc(last_var_made, 1)
                dve.wait_ge(last_rstd_guessed, 1)
                then(nc.vector.tensor_tensor(half, rstd, rstd, ALU.mult))
                then(nc.vector.tensor_tensor(half, half, var, ALU.mult))
                then(nc.vector.tensor_scalar(half, half, -0.5, 1.5, ALU.mult, ALU.add))
                then(nc.vector.tensor_tensor(rstd, half, rstd, ALU.mult))
                nc.vector.tensor_tensor(res[:], y[:], stretch(rstd, F), ALU.mult).then_inc(res_made, 1)

            for r in range(RB):
                make_mask(0, 0, 0, r, fresh=True)
            for g in range(G):
                for r in range(RB):
                    if g + 1 < G:
                        make_mask(0, 0, g + 1, r, fresh=True)
                    if r == 0:
                        dve.wait_ge(t_row_made, (g + 1) * T_SPREADS // G)
                    find_max(0, 0, g, r, fresh=True)
                    if g == G - 2 and r == RB - 1:
                        dve.wait_ge(ent_summed, 1)
                        nc.vector.tensor_copy(ent_sum[:], acc[:, 0, 0:FA]).then_inc(ent_kept, 1)
                    if g == G - 1 and r == 1:
                        keep_s(0)
            make_guard(0)
            for nth in range(2):
                leaky(0, 0, nth, fresh=True)
            superblock(0, 0, first=True)
            with dve.Fori(1, SB - 3, CYCLE) as s:
                for c in range(CYCLE):
                    superblock(s + c, (1 + c) % CYCLE)
            superblock(SB - 3, (SB - 3) % CYCLE)
            superblock(SB - 2, (SB - 2) % CYCLE, ahead=1)
            superblock(SB - 1, (SB - 1) % CYCLE, ahead=0)
            keep_acc(SB - 1)
            take_sums(SB - 1)
            finish_last(SB - 1)


def kernel(**inputs):
    import numpy as _np
    import concourse.bacc as _bacc
    from concourse.bass_utils import run_bass_kernel_spmd as _run

    names = ["x", "adj", "L0_gnn_entity_embs", "L0_gnn_W", "L0_gnn_a"]
    nc = _bacc.Bacc("TRN2", target_bir_lowering=False, num_devices=1)
    arrays, args = {}, []
    for name in names:
        v = _np.ascontiguousarray(inputs[name])
        arrays[f"in_{name}"] = v
        args.append(nc.dram_tensor(f"in_{name}", v.shape, mybir.dt.from_np(v.dtype), kind="ExternalInput").ap())
    out = nc.dram_tensor("out", inputs["x"].shape, F32, kind="ExternalOutput").ap()
    build_gat_layer(nc, *args, out)
    return _run(nc, [arrays], core_ids=[0]).results[0]["out"]
```
